# Optimizing a Trainium2 kernel written in Bass

```python
import numpy as np
import jax
import jax.numpy as jnp

def _softmax(x, axis=-1):
    return jax.nn.softmax(x, axis=axis)

def _gelu(x):
    return jax.nn.gelu(x, approximate=True)

def _silu(x):
    return jax.nn.silu(x)

def _sigmoid(x):
    return jax.nn.sigmoid(x)

def _layernorm(x, axis=-1, eps=1e-05):
    m = jnp.mean(x, axis=axis, keepdims=True)
    v = jnp.var(x, axis=axis, keepdims=True)
    return (x - m) / jnp.sqrt(v + eps)

def _scatter_add(tgt, idx, src, axis=0):
    return tgt.at[idx].add(src)

def _segment_sum(src, seg, n):
    return jax.ops.segment_sum(src, seg, n)
kernel_name = 'mk_macaron_d1_jaxref_r8_1d2403'

def setup_inputs(seed: int=0):
    np.random.seed(seed)
    _w = jnp.asarray

    def _L0_attn_setup():
        import jax, jax.numpy as jnp
        import numpy as np
        FP32_EPS = 1.1920929e-07

        def rms_norm(x):
            return x * jax.lax.rsqrt(jnp.mean(x * x, axis=-1, keepdims=True) + FP32_EPS)
        key = jax.random.key(seed)
        k1, k2, k3, k4 = jax.random.split(key, 4)
        n_embd, n_qkv = (128, 128)
        B, T = (4, 1024)

        def casted_init(k, out_f, in_f):
            s = 3.0 ** 0.5 * in_f ** (-0.5)
            return jax.random.uniform(k, (out_f, in_f), jnp.float32, -s, s)
        return {'x': jax.random.normal(k1, (B, T, n_embd), jnp.float32), 'w_qkv': casted_init(k2, 3 * n_qkv, n_embd), 'w_swiglu': casted_init(k3, 2 * n_embd, n_qkv), 'w_out': casted_init(k4, n_embd, n_embd)}
    _L0_attn_in = _L0_attn_setup()

    def _L0_ffn_setup():
        import jax, jax.numpy as jnp
        import numpy as np
        B, S, D, F, E, NS, K = (2, 128, 128, 512, 8, 8, 2)
        FS = F // NS
        key = jax.random.key(seed)
        ks = jax.random.split(key, 8)
        scale = 0.02
        return {'hidden_states': jax.random.normal(ks[0], (B, S, D), jnp.float32), 'gate_W': jax.random.normal(ks[1], (E, D), jnp.float32) * scale, 'w1_e': jax.random.normal(ks[2], (E, D, F), jnp.float32) * scale, 'w3_e': jax.random.normal(ks[3], (E, D, F), jnp.float32) * scale, 'w2_e': jax.random.normal(ks[4], (E, F, D), jnp.float32) * scale, 'w1_s': jax.random.normal(ks[5], (NS, D, FS), jnp.float32) * scale, 'w3_s': jax.random.normal(ks[6], (NS, D, FS), jnp.float32) * scale, 'w2_s': jax.random.normal(ks[7], (NS, FS, D), jnp.float32) * scale}
    _L0_ffn_in = _L0_ffn_setup()
    _d = {'L0_attn_x': _L0_attn_in['x'], 'L0_attn_w_qkv': _L0_attn_in['w_qkv'], 'L0_attn_w_swiglu': _L0_attn_in['w_swiglu'], 'L0_attn_w_out': _L0_attn_in['w_out'], 'L0_ffn_gate_W': _L0_ffn_in['gate_W'], 'L0_ffn_w1_e': _L0_ffn_in['w1_e'], 'L0_ffn_w3_e': _L0_ffn_in['w3_e'], 'L0_ffn_w2_e': _L0_ffn_in['w2_e'], 'L0_ffn_w1_s': _L0_ffn_in['w1_s'], 'L0_ffn_w3_s': _L0_ffn_in['w3_s'], 'L0_ffn_w2_s': _L0_ffn_in['w2_s']}
    _x0 = _d['L0_attn_x']
    _d['L0_attn_x'] = jax.random.normal(jax.random.fold_in(jax.random.key(seed), 1), (16, 256, 128), dtype=_x0.dtype)
    del _x0
    return _d

def reference(L0_attn_x, L0_attn_w_qkv, L0_attn_w_swiglu, L0_attn_w_out, L0_ffn_gate_W, L0_ffn_w1_e, L0_ffn_w3_e, L0_ffn_w2_e, L0_ffn_w1_s, L0_ffn_w3_s, L0_ffn_w2_s):

    def _L0_attn_ref(x, w_qkv, w_swiglu, w_out):
        import jax, jax.numpy as jnp
        import numpy as np
        FP32_EPS = 1.1920929e-07

        def rms_norm(x):
            return x * jax.lax.rsqrt(jnp.mean(x * x, axis=-1, keepdims=True) + FP32_EPS)
        qkv = jnp.einsum('btd,ed->bte', rms_norm(x), w_qkv)
        q, k, v = jnp.split(qkv, 3, axis=-1)
        q = rms_norm(q)
        k = rms_norm(k)
        w = jnp.exp(k)
        kv = w * v
        w = jnp.cumsum(w, axis=1)
        kv = jnp.cumsum(kv, axis=1)
        y = kv / (w + 1e-06)
        y = jax.nn.sigmoid(q) * y
        uv = jnp.einsum('bte,fe->btf', y, w_swiglu)
        u, g = jnp.split(uv, 2, axis=-1)
        return x + jnp.einsum('btd,ed->bte', u * jax.nn.silu(g), w_out)

    def _L0_ffn_ref(hidden_states, gate_W, w1_e, w3_e, w2_e, w1_s, w3_s, w2_s):
        import jax, jax.numpy as jnp
        import numpy as np
        B, S, D, F, E, NS, K = (2, 128, 128, 512, 8, 8, 2)
        FS = F // NS
        b, s, d = hidden_states.shape
        e = gate_W.shape[0]
        flat = hidden_states.reshape(-1, d)
        T = flat.shape[0]
        logits = (flat @ gate_W.T).astype(jnp.float32)
        probs = jax.nn.softmax(logits, axis=-1)
        top_v, top_i = jax.lax.top_k(probs, K)
        gates = jnp.zeros((T, e), probs.dtype).at[jnp.arange(T)[:, None], top_i].set(top_v)
        g = jax.nn.silu(jnp.einsum('td,edf->etf', flat, w1_e))
        u = jnp.einsum('td,edf->etf', flat, w3_e)
        out_e = jnp.einsum('etf,efd->etd', g * u, w2_e)
        routed = jnp.einsum('te,etd->td', gates, out_e).reshape(b, s, d)
        gs = jax.nn.silu(jnp.einsum('bsd,ndf->nbsf', hidden_states, w1_s))
        us = jnp.einsum('bsd,ndf->nbsf', hidden_states, w3_s)
        shared = jnp.einsum('nbsf,nfd->bsd', gs * us, w2_s) / w1_s.shape[0]
        alpha = 0.5
        return alpha * shared + (1.0 - alpha) * routed
    x = L0_attn_x
    x = x + 0.5 * _L0_ffn_ref(_layernorm(x, axis=-1), L0_ffn_gate_W, L0_ffn_w1_e, L0_ffn_w3_e, L0_ffn_w2_e, L0_ffn_w1_s, L0_ffn_w3_s, L0_ffn_w2_s)
    x = x + _L0_attn_ref(_layernorm(x, axis=-1), L0_attn_w_qkv, L0_attn_w_swiglu, L0_attn_w_out)
    x = x + 0.5 * _L0_ffn_ref(_layernorm(x, axis=-1), L0_ffn_gate_W, L0_ffn_w1_e, L0_ffn_w3_e, L0_ffn_w2_e, L0_ffn_w1_s, L0_ffn_w3_s, L0_ffn_w2_s)
    return x

_drawn_inputs = setup_inputs


def setup_inputs(seed=0):
    import zlib

    import numpy as np

    out = dict(_drawn_inputs(seed))
    spreads = {}
    factors = {'L0_attn_w_qkv': 5.879,
     'L0_attn_w_swiglu': 5.195,
     'L0_attn_w_out': 5.105,
     'L0_ffn_gate_W': 8.0,
     'L0_ffn_w1_e': 8.0,
     'L0_ffn_w3_e': 8.0,
     'L0_ffn_w2_e': 8.0,
     'L0_ffn_w1_s': 8.0,
     'L0_ffn_w3_s': 8.0,
     'L0_ffn_w2_s': 8.0}
    for name, (base, spread) in spreads.items():
        noise = np.random.default_rng([zlib.crc32(name.encode()), seed]).standard_normal(out[name].shape)
        drawn = base * np.exp(spread * noise) if base else spread * noise
        out[name] = jnp.asarray(drawn.astype(out[name].dtype))
    for name, factor in factors.items():
        out[name] = (out[name] * factor).astype(out[name].dtype)
    return out
```

```python
import concourse.bass as bass
from concourse import mybir
from contextlib import ExitStack

P = 128
D = 128
NT = 4096
TILES = NT // P
E = 8
TOPK = 2
F = 512
FT = F // P
CH = 4
CHUNKS = TILES // CH
SEQ = 256
BATCHES = NT // SEQ
TB = SEQ // P
TILES_R = TOPK * NT // P + E
GT = 4
GROUPS = TILES_R // GT
ROW = D + 2
LN_EPS = 1e-5
RMS_EPS = 1.1920929e-07
NS = 8

fp32 = mybir.dt.float32
bf16 = mybir.dt.bfloat16
i32 = mybir.dt.int32
ALU = mybir.AluOpType
ACT = mybir.ActivationFunctionType
X_AXIS = mybir.AxisListType.X


class Step:

    def __init__(self, r, u, unroll, first):
        self.r, self.u, self.unroll, self.first = r, u, unroll, first
        self.i = r * unroll + u

    def past(self, n):
        return self.first >= n or not isinstance(self.r, int)

    def over(self, n):
        return self.r * (self.unroll // n) + self.u // n


def pipelined(eng, stages, count, unroll, guard=2, at=None):
    deepest = max(d for _, d in stages)
    head = -(-(deepest + guard) // unroll) * unroll

    def static(k):
        if at and k in at:
            at[k]()
        for stage, d in stages:
            i = k - d
            if 0 <= i < count:
                stage(Step(i // unroll, i % unroll, unroll, i))

    for k in range(min(head, count)):
        static(k)
    if count > head:
        with eng.Fori(0, (count - head) // unroll) as r:
            for u in range(unroll):
                for stage, d in stages:
                    k = head + u - d
                    stage(Step(r + k // unroll, k % unroll, unroll, k))
    for k in range(count, count + deepest):
        static(k)


class Chain:

    def __init__(self, eng, sem):
        self.eng, self.sem, self.n = eng, sem, 0

    def then(self, instruction):
        instruction.then_inc(self.sem, 1)
        self.n += 1
        self.eng.wait_ge(self.sem, self.n)


def macaron(nc, x, w_qkvT, w_swigluT, w_outT, gateT, w1_e, w3_e, w2_e, w1_s, w3_s, w2_s, out):
    ctx = ExitStack()
    with ctx:
        def sb(name, shape, dt=fp32):
            return ctx.enter_context(nc.sbuf_tensor(name, shape, dt))

        def ps(name, shape, dt=fp32):
            return ctx.enter_context(nc.psum_tensor(name, shape, dt))

        def sem(name):
            return ctx.enter_context(nc.semaphore(name))

        slots = [nc.dram_tensor(f"slots{l}", [TILES_R * P, ROW], fp32, kind="Internal").ap() for l in range(2)]
        results = nc.dram_tensor("results", [(TOPK * TILES + TILES_R) * P, D], fp32, kind="Internal").ap()

        X = sb("X", [P, TILES, D])
        XN = sb("XN", [P, TILES, ROW])
        XNT = sb("XNT", [P, NT])
        W1 = sb("W1", [P, E * F])
        W3 = sb("W3", [P, E * F])
        W2 = sb("W2", [P, E * FT * D])
        W1S = sb("W1S", [P, F])
        W3S = sb("W3S", [P, F])
        W2S = sb("W2S", [P, FT, D])
        GATE = sb("GATE", [P, P])
        WQKV = sb("WQKV", [P, 3 * D])
        WSW = sb("WSW", [P, 2 * D])
        WOUT = sb("WOUT", [P, D])
        ident = sb("ident", [P, P])
        ones = sb("ones", [P, P])
        upto = sb("upto", [P, P])
        before = sb("before", [P, P], bf16)
        ones16 = sb("ones16", [P, P], bf16)
        rev_e = sb("rev_e", [P, E])
        tile_starts = sb("tile_starts", [P, TILES])
        tile_no = sb("tile_no", [P, TILES_R])
        slot_no = sb("slot_no", [P, TILES_R])
        targets = sb("targets", [P, TOPK, TILES], i32)
        pad_rows = sb("pad_rows", [P, ROW])
        minus_half = sb("minus_half", [P, 4])
        qk_factor = sb("qk_factor", [P, 2, TB])
        one_row = sb("one_row", [P, E * TILES])
        ln_stats = sb("ln_stats", [P, 2, CH, 6])
        ln_mv = sb("ln_mv", [P, 2, CH, 2])
        ln_var = sb("ln_var", [P, 2, CH])
        ln_rstd = sb("ln_rstd", [P, 2, CH])
        logit = sb("logit", [P, TILES, E])
        prob = sb("prob", [P, TILES, E])
        cand = sb("cand", [P, TILES, E])
        onehot = [sb(f"onehot{k}", [P, TILES, E]) for k in range(TOPK)]
        chosen16 = sb("chosen16", [P, TILES, E], bf16)
        row_a = sb("row_a", [P, TILES])
        row_b = sb("row_b", [P, TILES])
        top = [sb(f"top{k}", [P, TILES]) for k in range(TOPK)]
        tot = sb("tot", [P, E, TILES])
        cum = sb("cum", [P, E, TILES])
        excl = sb("excl", [P, E, TILES])
        pick = sb("pick", [P, E, TILES])
        cnt = sb("cnt", [P, E])
        need = sb("need", [P, E, TILES])
        ntile = sb("ntile", [P, E])
        tend = sb("tend", [P, E])
        tstart = sb("tstart", [P, E])
        shift = sb("shift", [P, E])
        tile_cmp = sb("tile_cmp", [P, TILES_R, E])
        tile_e = sb("tile_e", [P, TILES_R])
        w_off = sb("w_off", [P, TILES_R], i32)
        posf = sb("posf", [P, TILES])
        pos = [sb(f"pos{k}", [P, TILES], i32) for k in range(TOPK)]
        silu = sb("silu", [P, 2, F])
        hs = sb("hs", [P, 2, FT, CH * P])
        rows = sb("rows", [P, 2, GT, ROW])
        xT = sb("xT", [P, 2, GT, P])
        tile_gate = sb("tile_gate", [P, 2, GT])
        own_row = sb("own_row", [P, 2, GT])
        tile_tgt = sb("tile_tgt", [P, 2, GT], i32)
        hr = sb("hr", [P, 2, F])
        hT = sb("hT", [P, 2, FT, P])
        yout = sb("yout", [P, 2, GT, D])
        ytgt = sb("ytgt", [P, 2, GT], i32)
        Y = sb("Y", [P, 2, TOPK, TB, D])
        at_stats = sb("at_stats", [P, 2, TB, 6])
        at_mv = sb("at_mv", [P, 2, TB, 2])
        at_var = sb("at_var", [P, 2, TB])
        at_rstd = sb("at_rstd", [P, 2, TB])
        at_ms = sb("at_ms", [P, 2, 4, TB])
        at_rr = sb("at_rr", [P, 2, TB])
        xr = sb("xr", [P, 2, TB, D])
        xn = sb("xn", [P, 2, TB, D])
        xrT = sb("xrT", [P, 2, TB * P])
        sq = sb("sq", [P, 2, 2, TB, D])
        qk_ss = sb("qk_ss", [P, 2, 2, TB])
        qk_ms = sb("qk_ms", [P, 2, 3, 2, TB])
        wkv = sb("wkv", [P, 2, TB, 2, D])
        tq = sb("tq", [P, 2, TB, D])
        den = sb("den", [P, 2, TB, D])
        rec = sb("rec", [P, 2, TB, D])
        ysc = sb("ysc", [P, 2, TB, D])
        ya = sb("ya", [P, 2, TB, D])
        yT = sb("yT", [P, 2, TB * P])
        tg = sb("tg", [P, 2, TB * P])
        ag = sb("ag", [P, 2, TB * P])
        ha = sb("ha", [P, 2, TB * P])

        psG = ps("psG", [P, 2, 512])
        psU = ps("psU", [P, 2, 512])
        psH = ps("psH", [P, 2, 512])
        psT = ps("psT", [P, 512])
        psY = ps("psY", [P, 512])

        x_in = [sem(f"x_in{c}") for c in range(CHUNKS)]
        small_in = sem("small_in")
        experts_in = sem("experts_in")
        attn_in = sem("attn_in")
        padded = [sem(f"padded{l}") for l in range(2)]
        consts = sem("consts")
        const_link = sem("const_link")
        ln_link = sem("ln_link")
        ln_stat = sem("ln_stat")
        ln_scaled = sem("ln_scaled")
        xn_done = sem("xn_done")
        xnT_psum = sem("xnT_psum")
        xnT_done = sem("xnT_done")
        logits_done = sem("logits_done")
        logits_out = sem("logits_out")
        route_link = sem("route_link")
        shifted = sem("shifted")
        expd = sem("expd")
        picked = sem("picked")
        ranked = sem("ranked")
        ranks_read = sem("ranks_read")
        w_off_done = sem("w_off_done")
        pos_done = sem("pos_done")
        sent = [sem(f"sent{k}") for k in range(TOPK)]
        retarget = sem("retarget")
        g_full = sem("g_full")
        u_full = sem("u_full")
        silu_done = sem("silu_done")
        h_done = sem("h_done")
        sh_full = sem("sh_full")
        sh_added = sem("sh_added")
        rows_in = [sem(f"rows_in{p}") for p in range(2)]
        xT_psum = sem("xT_psum")
        xT_done = sem("xT_done")
        tgt_link = sem("tgt_link")
        hT_psum = sem("hT_psum")
        hT_done = sem("hT_done")
        y_psum = sem("y_psum")
        y_done = sem("y_done")
        y_sent = [sem(f"y_sent{p}") for p in range(2)]
        y_in = [sem(f"y_in{p}") for p in range(2)]
        add_link = sem("add_link")
        routed_added = sem("routed_added")
        half_added = sem("half_added")
        out_sent = sem("out_sent")
        at_link = sem("at_link")
        at_stat = sem("at_stat")
        pool_link = sem("pool_link")
        at_scaled = sem("at_scaled")
        xr_done = sem("xr_done")
        xres_done = sem("xres_done")
        xrT_psum = sem("xrT_psum")
        xrT_done = sem("xrT_done")
        qkv_psum = sem("qkv_psum")
        ss_done = sem("ss_done")
        qk_scaled = sem("qk_scaled")
        w_done = sem("w_done")
        qk_link = sem("qk_link")
        kv_done = sem("kv_done")
        cum_psum = sem("cum_psum")
        y_link = sem("y_link")
        ya_done = sem("ya_done")
        yT_psum = sem("yT_psum")
        yT_done = sem("yT_done")
        uv_psum = sem("uv_psum")
        tg_done = sem("tg_done")
        h_link = sem("h_link")
        ha_done = sem("ha_done")
        at_psum = sem("at_psum")
        at_added = sem("at_added")

        block = ctx.enter_context(nc.Block())
        CONSTS = 14
        SHARED = CHUNKS * FT
        first_shared = [l * (SHARED + TILES_R) for l in range(2)]
        first_routed = [f + SHARED for f in first_shared]

        def wait_apart(eng, semaphore, value):
            if isinstance(value, int):
                eng.wait_ge(semaphore, value)
                return
            with eng.register() as wanted:
                eng.reg_mov(wanted, value)
                eng.wait_ge(consts, CONSTS)
                eng.wait_ge(semaphore, wanted)

        x_v = x.rearrange("(i p) d -> p i d", p=P)
        out_v = out.rearrange("(i p) d -> p i d", p=P)
        results_v = results[0:TOPK * NT, :].rearrange("(k i p) d -> p k i d", k=TOPK, p=P)

        @block.sync
        def _(sp):
            for c in range(CHUNKS):
                sp.dma_start(X[:, c * CH:(c + 1) * CH, :], x_v[:, c * CH:(c + 1) * CH, :]).then_inc(x_in[c], 16)
                if c == 1:
                    for dst, src in ((GATE[:, :], gateT), (W1S[:, :], w1_s), (W3S[:, :], w3_s),
                                     (W2S[:, :, :], w2_s.rearrange("(j p) d -> p j d", p=P))):
                        sp.dma_start(dst, src).then_inc(small_in, 16)
            sp.wait_ge(consts, CONSTS)
            for l in range(2):
                if l == 1:
                    for dst, src in ((W1[:, :], w1_e), (W3[:, :], w3_e),
                                     (W2[:, :], w2_e)):
                        sp.dma_start(dst, src).then_inc(experts_in, 16)
                    for dst, src in ((WQKV[:, :], w_qkvT), (WSW[:, :], w_swigluT), (WOUT[:, :], w_outT)):
                        sp.dma_start(dst, src).then_inc(attn_in, 16)
                sp.dma_start(slots[l].rearrange("(j p) c -> p j c", p=P),
                             pad_rows[:, :].unsqueeze(1).to_broadcast([P, TILES_R, ROW])).then_inc(padded[l], 16)
            for l in range(2):
                slots_v = slots[l].rearrange("(g t p) c -> g p t c", t=GT, p=P)
                for k in range(TOPK):
                    sp.wait_ge(sent[k], 16 * TILES * (l + 1))

                def load_rows(s):
                    if s.past(2):
                        sp.wait_ge(xT_done, s.i + (l * GROUPS - 1))
                    sp.dma_start(rows[:, s.u, :, :], slots_v[bass.ds(s.i, 1), :, :, :].squeeze(0)
                                 if not isinstance(s.i, int) else slots_v[s.i, :, :, :]).then_inc(rows_in[s.u], 16)

                pipelined(sp, [(load_rows, 0)], GROUPS, 2)
                for p in range(2):
                    sp.wait_ge(y_sent[p], 16 * TILES_R // 2 * (l + 1))

                def load_results(s):
                    if s.past(2):
                        sp.wait_ge(routed_added, s.i + (l * BATCHES - 1))
                    for k in range(TOPK):
                        sp.dma_start(Y[:, s.u, k, :, :], results_v[:, k, bass.ds(s.i * TB, TB), :])\
                          .then_inc(y_in[s.u], 16)

                pipelined(sp, [(load_results, 0)], BATCHES, 2)

        @block.gpsimd
        def _(pool):
            one = Chain(pool, const_link)
            pool.memset(ones[:, :], 1.0).then_inc(consts, 1)
            pool.memset(ones16[:, :], 1.0).then_inc(consts, 1)
            pool.memset(minus_half[:, :], -0.5).then_inc(consts, 1)
            pool.memset(one_row[:, :], 1.0).then_inc(consts, 1)
            one.then(pool.memset(ident[:, :], 0.0))
            one.then(pool.memset(upto[:, :], 1.0))
            one.then(pool.memset(before[:, :], 1.0))
            one.then(pool.memset(pad_rows[:, :], 0.0))
            one.then(pool.memset(qk_factor[:, :, :], 1.0))
            pool.affine_select(out=ident[:, :], in_=ident[:, :], compare_op=ALU.not_equal, fill=1.0,
                               base=0, pattern=[[-1, P]], channel_multiplier=1).then_inc(consts, 1)
            pool.affine_select(out=upto[:, :], in_=upto[:, :], compare_op=ALU.is_ge, fill=0.0,
                               base=0, pattern=[[1, P]], channel_multiplier=-1).then_inc(consts, 1)
            pool.affine_select(out=before[:, :], in_=before[:, :], compare_op=ALU.is_gt, fill=0.0,
                               base=0, pattern=[[1, P]], channel_multiplier=-1).then_inc(consts, 1)
            pool.iota(slot_no[:, :], pattern=[[P, TILES_R]], base=0, channel_multiplier=1,
                      allow_small_or_imprecise_dtypes=True).then_inc(consts, 1)
            pool.iota(pad_rows[:, D + 1:D + 2].bitcast(i32), pattern=[[0, 1]], base=TOPK * NT,
                      channel_multiplier=0).then_inc(consts, 1)
            pool.memset(qk_factor[:, 0, :], 0.5).then_inc(consts, 1)
            pool.iota(rev_e[:, :], pattern=[[-1, E]], base=E, channel_multiplier=0,
                      allow_small_or_imprecise_dtypes=True).then_inc(consts, 1)
            pool.iota(tile_starts[:, :], pattern=[[P, TILES]], base=0, channel_multiplier=0,
                      allow_small_or_imprecise_dtypes=True).then_inc(consts, 1)
            pool.iota(tile_no[:, :], pattern=[[1, TILES_R]], base=0, channel_multiplier=0,
                      allow_small_or_imprecise_dtypes=True).then_inc(consts, 1)
            pool.iota(targets[:, :, :], pattern=[[NT, TOPK], [P, TILES]], base=0,
                      channel_multiplier=1).then_inc(consts, 1)
            pool.wait_ge(consts, CONSTS)

            def add_routed(l):
                def run(s):
                    xs = X[:, bass.ds(s.i * TB, TB), :]
                    wait_apart(pool, y_in[s.u], 16 * TOPK * (s.over(2) + (l * BATCHES // 2 + 1)))
                    if s.first == 0:
                        pool.wait_ge(sh_added, CHUNKS * (l + 1))
                    pool.tensor_tensor(xs, xs, Y[:, s.u, 0, :, :], ALU.add).then_inc(add_link, 1)
                    wait_apart(pool, add_link, s.i + (l * BATCHES + 1))
                    pool.tensor_tensor(xs, xs, Y[:, s.u, 1, :, :], ALU.add).then_inc(routed_added, 1)
                return run

            for l in range(2):
                def scale_ln(s):
                    pool.wait_ge(ln_stat, s.i + (l * CHUNKS + 1))
                    pool.tensor_tensor(ln_rstd[:, s.u, :], ln_var[:, s.u, :], minus_half[:, :], ALU.pow)\
                        .then_inc(ln_scaled, 1)

                pipelined(pool, [(scale_ln, 0)], CHUNKS, 2)
                pool.wait_ge(padded[l], 16)
                for k in range(TOPK):
                    pool.wait_ge(pos_done, TOPK * l + k + 1)
                    for i in range(TILES):
                        pool.indirect_dma_start(slots[l], bass.IndirectOffsetOnAxis(ap=pos[k][:, i:i + 1], axis=0),
                                                XN[:, i, :], None).then_inc(sent[k], 16)

                def send_results(s):
                    wait_apart(pool, y_done, s.i + (l * GROUPS + 1))
                    for t in range(GT):
                        pool.indirect_dma_start(
                            results, bass.IndirectOffsetOnAxis(ap=ytgt[:, s.u, t:t + 1], axis=0),
                            yout[:, s.u, t, :], None).then_inc(y_sent[s.u], 16)

                pipelined(pool, [(send_results, 0)], GROUPS, 2)

                def scale_at(s):
                    link = s.i * 5
                    pool.wait_ge(at_stat, s.i + 1)
                    rstd, var = at_rstd[:, s.u, :], at_mv[:, s.u, :, 1]
                    ms = [at_ms[:, s.u, j, :] for j in range(4)]
                    pool.tensor_tensor(rstd, at_var[:, s.u, :], minus_half[:, 0:TB], ALU.pow).then_inc(pool_link, 1)
                    pool.wait_ge(pool_link, link + 1)
                    pool.tensor_tensor(ms[0], rstd, rstd, ALU.mult).then_inc(pool_link, 1)
                    pool.wait_ge(pool_link, link + 2)
                    pool.tensor_tensor(ms[1], ms[0], var, ALU.mult).then_inc(pool_link, 1)
                    wait_apart(pool, pool_link, link + 3)
                    pool.tensor_scalar(ms[2], ms[1], RMS_EPS, None, ALU.add).then_inc(pool_link, 1)
                    pool.wait_ge(pool_link, link + 4)
                    pool.tensor_tensor(ms[3], ms[2], minus_half[:, 0:TB], ALU.pow).then_inc(pool_link, 1)
                    pool.wait_ge(pool_link, link + 5)
                    pool.tensor_tensor(at_rr[:, s.u, :], ms[3], rstd, ALU.mult).then_inc(at_scaled, 1)

                def residual(s):
                    wait_apart(pool, xr_done, s.i + 1)
                    xs = X[:, bass.ds(s.i * TB, TB), :]
                    pool.tensor_tensor(xs, xs, xn[:, s.u, :, :], ALU.add).then_inc(xres_done, 1)

                def scale_qk(s):
                    link = s.i * 2
                    wait_apart(pool, ss_done, s.i + 1)
                    ms = [qk_ms[:, s.u, j, :, :] for j in range(3)]
                    pool.tensor_scalar(ms[0], qk_ss[:, s.u, :, :], 1.0 / D, RMS_EPS, ALU.mult, ALU.add)\
                        .then_inc(qk_link, 1)
                    pool.wait_ge(qk_link, link + 1)
                    pool.tensor_tensor(ms[1], ms[0], minus_half[:, :].rearrange("p (a b) -> p a b", a=2), ALU.pow)\
                        .then_inc(qk_link, 1)
                    pool.wait_ge(qk_link, link + 2)
                    pool.tensor_tensor(ms[2], ms[1], qk_factor[:, :, :], ALU.mult).then_inc(qk_scaled, 1)

                if l == 0:
                    pipelined(pool, [(scale_qk, 2), (add_routed(0), 0), (residual, 1), (scale_at, 0)], BATCHES, 2)
                else:
                    pipelined(pool, [(add_routed(1), 0)], BATCHES, 2)

        @block.vector
        def _(dve):
            dve.wait_ge(consts, CONSTS)
            route = Chain(dve, route_link)

            def wide(ap, shape):
                return ap.unsqueeze(2).to_broadcast(shape)

            TE = [P, TILES, E]
            ET = [P, E, TILES]
            for l in range(2):
                def stats(s):
                    if l == 0:
                        dve.wait_ge(x_in[s.i], 16)
                    elif s.first == 0:
                        dve.wait_ge(at_added, BATCHES)
                    base = 2 * CHUNKS * l
                    for t in range(CH):
                        i = dve.bn_stats(ln_stats[:, s.u % 2, t, :], X[:, s.i * CH + t, :])
                    i.then_inc(ln_link, 1)
                    dve.wait_ge(ln_link, base + 2 * s.i + 1)
                    for t in range(CH):
                        i = dve.bn_aggr(ln_mv[:, s.u % 2, t, :], ln_stats[:, s.u % 2, t, :])
                    i.then_inc(ln_link, 1)
                    dve.wait_ge(ln_link, base + 2 * s.i + 2)
                    dve.tensor_scalar(ln_var[:, s.u % 2, :], ln_mv[:, s.u % 2, :, 1], LN_EPS, None, ALU.add)\
                       .then_inc(ln_stat, 1)

                def normalise(s):
                    dve.wait_ge(ln_scaled, s.i + (l * CHUNKS + 1))
                    for t in range(CH):
                        i = dve.tensor_scalar(XN[:, s.i * CH + t, 0:D], X[:, s.i * CH + t, :],
                                              ln_mv[:, s.u % 2, t, 0:1], ln_rstd[:, s.u % 2, t:t + 1],
                                              ALU.subtract, ALU.mult)
                    i.then_inc(xn_done, 1)

                for c in range(CHUNKS + 1):
                    if c < CHUNKS:
                        stats(Step(c // 2, c % 2, 2, c))
                    if c > 0:
                        normalise(Step((c - 1) // 2, (c - 1) % 2, 2, c - 1))

                for c in range(CHUNKS):
                    dve.wait_ge(logits_done, CHUNKS * l + c + 1)
                    i = dve.tensor_copy(logit[:, c * CH:(c + 1) * CH, :],
                                        psY[:, :].rearrange("p (t e) -> p t e", t=CH)[:, :, 0:E])
                    i.then_inc(logits_out, 1)
                dve.wait_ge(logits_out, CHUNKS * (l + 1))
                route.then(dve.tensor_reduce(row_a[:, :], logit[:, :, :], X_AXIS, ALU.max))
                dve.tensor_tensor(cand[:, :, :], logit[:, :, :], wide(row_a[:, :], TE), ALU.subtract)\
                   .then_inc(shifted, 1)
                dve.wait_ge(expd, l + 1)
                route.then(dve.tensor_reduce(row_b[:, :], prob[:, :, :], X_AXIS, ALU.add))
                route.then(dve.reciprocal(row_a[:, :], row_b[:, :]))
                route.then(dve.tensor_tensor(prob[:, :, :], prob[:, :, :], wide(row_a[:, :], TE), ALU.mult))
                for k in range(TOPK):
                    route.then(dve.tensor_reduce(top[k][:, :], prob[:, :, :], X_AXIS, ALU.max))
                    route.then(dve.tensor_tensor(cand[:, :, :], prob[:, :, :], wide(top[k][:, :], TE), ALU.is_ge))
                    route.then(dve.tensor_tensor(cand[:, :, :], cand[:, :, :],
                                                 rev_e[:, :].unsqueeze(1).to_broadcast(TE), ALU.mult))
                    route.then(dve.tensor_reduce(row_b[:, :], cand[:, :, :], X_AXIS, ALU.max))
                    route.then(dve.tensor_tensor(onehot[k][:, :, :], rev_e[:, :].unsqueeze(1).to_broadcast(TE),
                                                 wide(row_b[:, :], TE), ALU.is_equal))
                    if k == 0:
                        route.then(dve.scalar_tensor_tensor(prob[:, :, :], onehot[0][:, :, :], -2.0,
                                                            prob[:, :, :], ALU.mult, ALU.add))
                dve.tensor_tensor(chosen16[:, :, :], onehot[0][:, :, :], onehot[1][:, :, :], ALU.add)\
                   .then_inc(picked, 1)

                def slots_of():
                    dve.wait_ge(ranked, l + 1)
                    within = psY[:, 0:TILES * E].rearrange("p (i e) -> p e i", e=E)
                    totals = psY[:, TILES * E:2 * TILES * E].rearrange("p (i e) -> p e i", e=E)
                    route.then(dve.tensor_copy(tot[:, :, :], totals))
                    flat = "p e i -> p (e i)"
                    route.then(dve.tensor_tensor_scan(cum[:, :, :].rearrange(flat), one_row[:, :],
                                                      tot[:, :, :].rearrange(flat), 0.0, ALU.mult, ALU.add))
                    route.then(dve.tensor_tensor(excl[:, :, :], cum[:, :, :], tot[:, :, :], ALU.subtract))
                    route.then(dve.tensor_tensor(cnt[:, :], cum[:, :, TILES - 1], excl[:, :, 0], ALU.subtract))
                    route.then(dve.tensor_tensor(need[:, :, :], wide(cnt[:, :], ET),
                                                 tile_starts[:, :].unsqueeze(1).to_broadcast(ET), ALU.is_gt))
                    route.then(dve.tensor_reduce(ntile[:, :], need[:, :, :], X_AXIS, ALU.add))
                    route.then(dve.tensor_tensor_scan(tend[:, :], one_row[:, 0:E], ntile[:, :], 0.0,
                                                      ALU.mult, ALU.add))
                    route.then(dve.tensor_tensor(tstart[:, :], tend[:, :], ntile[:, :], ALU.subtract))
                    route.then(dve.scalar_tensor_tensor(shift[:, :], tstart[:, :], float(P), excl[:, :, 0],
                                                        ALU.mult, ALU.subtract))
                    route.then(dve.tensor_tensor(excl[:, :, :], excl[:, :, :], wide(shift[:, :], ET), ALU.add))
                    i = dve.tensor_tensor(excl[:, :, :], excl[:, :, :], within, ALU.add)
                    i.then_inc(ranks_read, 1)
                    dve.wait_ge(ranks_read, l + 1)
                    for k in range(TOPK):
                        route.then(dve.tensor_tensor(pick[:, :, :], excl[:, :, :],
                                                     onehot[k][:, :, :].rearrange("p i e -> p e i"), ALU.mult))
                        route.then(dve.tensor_reduce(posf[:, :], pick[:, :, :].rearrange("p e i -> p i e"),
                                                     X_AXIS, ALU.add))
                        route.then(dve.tensor_copy(pos[k][:, :], posf[:, :]))
                        if k == 1:
                            dve.wait_ge(sent[0], 16 * TILES * (l + 1))
                        route.then(dve.tensor_scalar(XN[:, :, D], top[k][:, :], 0.25, None, ALU.mult))
                        dve.tensor_copy(XN[:, :, D + 1].bitcast(i32), targets[:, k, :]).then_inc(pos_done, 1)
                        if k == 0:
                            cmp3 = [P, TILES_R, E]
                            route.then(dve.tensor_tensor(tile_cmp[:, :, :], wide(tile_no[:, :], cmp3),
                                                         tend[:, :].unsqueeze(1).to_broadcast(cmp3), ALU.is_ge))
                            route.then(dve.tensor_reduce(tile_e[:, :], tile_cmp[:, :, :], X_AXIS, ALU.add))
                            dve.tensor_scalar(w_off[:, :], tile_e[:, :], float(E - 1), float(F),
                                              ALU.min, ALU.mult).then_inc(w_off_done, 1)
                            for m in range(3):
                                gated_shared(Step(0, m, 2 * FT, m))

                def gated(hidden, s, base):
                    dve.wait_ge(silu_done, s.i + (base + 1))
                    dve.wait_ge(u_full, s.i + (base + 1))
                    dve.tensor_tensor(hidden, silu[:, s.u % 2, :], psU[:, s.u % 2, :], ALU.mult).then_inc(h_done, 1)

                def gated_shared(s):
                    if s.past(2 * FT) and s.u % FT == 0:
                        dve.wait_ge(sh_full, s.over(FT) + (CHUNKS * l - 1))
                    gated(hs[:, s.u // FT, s.u % FT, :], s, first_shared[l])

                def add_shared(s):
                    if s.u % FT:
                        return
                    c = s.over(FT)
                    dve.wait_ge(sh_full, c + (CHUNKS * l + 1))
                    xs = X[:, bass.ds(c * CH, CH), :].rearrange("p t d -> p (t d)")
                    dve.scalar_tensor_tensor(xs, psH[:, s.u // FT, :], 0.25 / NS, xs, ALU.mult, ALU.add)\
                       .then_inc(sh_added, 1)

                done = 3
                slots_of()

                def gated_rest(s):
                    if s.past(done):
                        gated_shared(s)

                pipelined(dve, [(gated_rest, 0), (add_shared, 6)], SHARED, 2 * FT)

                def gated_routed(s):
                    if s.past(2):
                        dve.wait_ge(hT_psum, s.i + (TILES_R * l - 1))
                    gated(hr[:, s.u % 2, :], s, first_routed[l])

                def copy_xT(s):
                    if s.u % GT:
                        return
                    g, par = s.over(GT), s.u // GT
                    dve.wait_ge(xT_psum, g + (GROUPS * l + 1))
                    if s.past(2 * GT):
                        dve.wait_ge(u_full, s.i + (first_routed[l] - GT))
                    dve.tensor_copy(xT[:, par, :, :].rearrange("p t c -> p (t c)"), psT[:, :])
                    dve.tensor_copy(tile_gate[:, par, :], rows[:, par, :, D])
                    target = rows[:, par, :, D + 1].bitcast(i32)
                    dve.scalar_tensor_tensor(own_row[:, par, :], target, float(TOPK * NT), slot_no[:, bass.ds(s.i, GT)],
                                             ALU.is_ge, ALU.mult).then_inc(tgt_link, 1)
                    dve.wait_ge(tgt_link, g + (GROUPS * l + 1))
                    dve.tensor_tensor(tile_tgt[:, par, :], own_row[:, par, :], target, ALU.add).then_inc(xT_done, 1)

                def scale_y(s):
                    if s.u % GT != GT - 1:
                        return
                    g, par = s.over(GT), s.u // GT
                    dve.wait_ge(y_psum, s.i + (TILES_R * l + 1))
                    dve.wait_ge(xT_done, g + (GROUPS * l + 1))
                    if s.past(2 * GT):
                        dve.wait_ge(y_sent[par], 16 * GT * (s.over(2 * GT) + l * GROUPS // 2))
                    for t in range(GT):
                        dve.tensor_scalar(yout[:, par, t, :], psY[:, t * D:(t + 1) * D],
                                          tile_gate[:, par, t:t + 1], None, ALU.mult)
                    dve.tensor_copy(ytgt[:, par, :], tile_tgt[:, par, :]).then_inc(y_done, 1)

                pipelined(dve, [(gated_routed, 2), (scale_y, 4), (copy_xT, 0)], TILES_R, 2 * GT)

                if l == 1:
                    continue

                def at_statistics(s):
                    dve.wait_ge(routed_added, s.i + 1)
                    for t in range(TB):
                        i = dve.bn_stats(at_stats[:, s.u, t, :],
                                         X[:, bass.ds(s.i * TB + t, 1), :].rearrange("p a d -> p (a d)"))
                    i.then_inc(at_link, 1)
                    wait_apart(dve, at_link, s.i * 2 + 1)
                    for t in range(TB):
                        i = dve.bn_aggr(at_mv[:, s.u, t, :], at_stats[:, s.u, t, :])
                    i.then_inc(at_link, 1)
                    dve.wait_ge(at_link, s.i * 2 + 2)
                    dve.tensor_scalar(at_var[:, s.u, :], at_mv[:, s.u, :, 1], LN_EPS, None, ALU.add)\
                       .then_inc(at_stat, 1)

                def at_normalise(s):
                    dve.wait_ge(at_scaled, s.i + 1)
                    if s.past(2):
                        dve.wait_ge(xrT_psum, s.i - 1)
                        dve.wait_ge(xres_done, s.i - 1)
                    for t in range(TB):
                        xt = X[:, bass.ds(s.i * TB + t, 1), :].rearrange("p a d -> p (a d)")
                        dve.tensor_scalar(xr[:, s.u, t, :], xt, at_mv[:, s.u, t, 0:1], at_rr[:, s.u, t:t + 1],
                                          ALU.subtract, ALU.mult)
                        i = dve.tensor_scalar(xn[:, s.u, t, :], xt, at_mv[:, s.u, t, 0:1],
                                              at_rstd[:, s.u, t:t + 1], ALU.subtract, ALU.mult)
                    i.then_inc(xr_done, 1)

                def weigh_v(s):
                    dve.wait_ge(w_done, s.i + 1)
                    dve.tensor_tensor(wkv[:, s.u, :, 1, :], wkv[:, s.u, :, 0, :], psG[:, :, 2 * D:3 * D],
                                      ALU.mult).then_inc(kv_done, 1)

                def attend(s):
                    dve.wait_ge(cum_psum, s.i + 1)
                    sums = psU[:, 0, :].rearrange("p (t a d) -> p t a d", t=TB, a=2)
                    dve.tensor_scalar(den[:, s.u, :, :], sums[:, :, 0, :], 2.0, 2e-6, ALU.mult, ALU.add)\
                       .then_inc(y_link, 1)
                    dve.wait_ge(y_link, s.i * 3 + 1)
                    dve.reciprocal(rec[:, s.u, :, :], den[:, s.u, :, :]).then_inc(y_link, 1)
                    dve.wait_ge(y_link, s.i * 3 + 2)
                    dve.scalar_tensor_tensor(ysc[:, s.u, :, :], tq[:, s.u, :, :], 1.0, rec[:, s.u, :, :],
                                             ALU.add, ALU.mult).then_inc(y_link, 1)
                    dve.wait_ge(y_link, s.i * 3 + 3)
                    if s.past(2):
                        dve.wait_ge(yT_psum, s.i - 1)
                    dve.tensor_tensor(ya[:, s.u, :, :], ysc[:, s.u, :, :], sums[:, :, 1, :], ALU.mult)\
                       .then_inc(ya_done, 1)

                def gate_u(s):
                    dve.wait_ge(tg_done, s.i + 1)
                    dve.scalar_tensor_tensor(ag[:, s.u, :], tg[:, s.u, :], 1.0, psU[:, 1, 256:512],
                                             ALU.add, ALU.mult).then_inc(h_link, 1)
                    dve.wait_ge(h_link, s.i + 1)
                    if s.past(2):
                        dve.wait_ge(at_psum, s.i - 1)
                    dve.tensor_tensor(ha[:, s.u, :], ag[:, s.u, :], psU[:, 1, 0:256], ALU.mult)\
                       .then_inc(ha_done, 1)

                def add_attention(s):
                    dve.wait_ge(at_psum, s.i + 1)
                    dve.wait_ge(xres_done, s.i + 1)
                    xs = X[:, bass.ds(s.i * TB, TB), :].rearrange("p t d -> p (t d)")
                    dve.scalar_tensor_tensor(xs, psT[:, 0:TB * D], 0.5, xs, ALU.mult, ALU.add)\
                       .then_inc(at_added, 1)

                pipelined(dve, [(weigh_v, 2), (gate_u, 4), (add_attention, 5), (at_normalise, 1),
                                (at_statistics, 0), (attend, 3)], BATCHES, 2)

        @block.scalar
        def _(act):
            act.wait_ge(consts, CONSTS)
            for l in range(2):
                def copy_xnT(s):
                    act.wait_ge(xnT_psum, s.i + (CHUNKS * l + 1))
                    act.activation(XNT[:, bass.ds(s.i * CH * P, CH * P)], psH[:, s.u, :], ACT.Copy)\
                       .then_inc(xnT_done, 1)

                pipelined(act, [(copy_xnT, 0)], CHUNKS, 2)
                act.wait_ge(shifted, l + 1)
                act.activation(prob[:, :, :], cand[:, :, :], ACT.Exp).then_inc(expd, 1)

                def silu_of(s, base):
                    act.wait_ge(g_full, s.i + (base + 1))
                    if s.first + base >= 2:
                        act.wait_ge(h_done, s.i + (base - 1))
                    act.activation(silu[:, s.u % 2, :], psG[:, s.u % 2, :], ACT.Silu).then_inc(silu_done, 1)

                pipelined(act, [(lambda s: silu_of(s, first_shared[l]), 0)], SHARED, 2)

                def copy_hT(s):
                    act.wait_ge(hT_psum, s.i + (TILES_R * l + 1))
                    if s.past(2):
                        act.wait_ge(y_psum, s.i + (TILES_R * l - 1))
                    act.activation(hT[:, s.u % 2, :, :].rearrange("p j c -> p (j c)"), psH[:, s.u % 2, :],
                                   ACT.Copy).then_inc(hT_done, 1)

                pipelined(act, [(lambda s: silu_of(s, first_routed[l]), 0), (copy_hT, 1)], TILES_R, 2)

                if l == 1:
                    def store(s):
                        act.wait_ge(routed_added, s.i + (BATCHES + 1))
                        act.dma_start(out_v[:, bass.ds(s.i * TB, TB), :], X[:, bass.ds(s.i * TB, TB), :])\
                           .then_inc(out_sent, 16)

                    pipelined(act, [(store, 0)], BATCHES, 2)
                    act.wait_ge(out_sent, 16 * BATCHES)
                    continue

                def copy_xrT(s):
                    act.wait_ge(xrT_psum, s.i + 1)
                    act.activation(xrT[:, s.u, :], psH[:, 0, 0:TB * P], ACT.Copy).then_inc(xrT_done, 1)

                def squares(s):
                    act.wait_ge(qkv_psum, s.i + 1)
                    for a in range(2):
                        for t in range(TB):
                            i = act.activation(sq[:, s.u, a, t, :], psG[:, t, a * D:(a + 1) * D], ACT.Square,
                                               accum_out=qk_ss[:, s.u, a, t:t + 1])
                    i.then_inc(ss_done, 1)

                def weights(s):
                    act.wait_ge(qk_scaled, s.i + 1)
                    if s.past(2):
                        act.wait_ge(ya_done, s.i - 1)
                    for t in range(TB):
                        act.activation(wkv[:, s.u, t, 0, :], psG[:, t, D:2 * D], ACT.Exp,
                                       scale=qk_ms[:, s.u, 2, 1, t:t + 1])
                    for t in range(TB):
                        i = act.activation(tq[:, s.u, t, :], psG[:, t, 0:D], ACT.Tanh,
                                           scale=qk_ms[:, s.u, 2, 0, t:t + 1])
                    i.then_inc(w_done, 1)

                def copy_yT(s):
                    act.wait_ge(yT_psum, s.i + 1)
                    act.activation(yT[:, s.u, :], psH[:, 1, 0:TB * P], ACT.Copy).then_inc(yT_done, 1)

                def tanh_g(s):
                    act.wait_ge(uv_psum, s.i + 1)
                    act.activation(tg[:, s.u, :], psU[:, 1, 256:512], ACT.Tanh, scale=0.5).then_inc(tg_done, 1)

                pipelined(act, [(copy_yT, 3), (tanh_g, 3), (weights, 1), (copy_xrT, 0), (squares, 0)],
                          BATCHES, 2)

        @block.tensor
        def _(pe):
            pe.wait_ge(consts, CONSTS)
            pe.wait_ge(small_in, 64)

            def table_entry(j):
                return pe.value_load(w_off[0:1, bass.ds(j, 1)], min_val=0, max_val=(E - 1) * F)

            for l in range(2):
                for c in range(CHUNKS + 1):
                    if c < CHUNKS:
                        pe.wait_ge(xn_done, CHUNKS * l + c + 1)
                        if c >= 2:
                            pe.wait_ge(xnT_done, CHUNKS * l + c - 1)
                        for t in range(CH):
                            i = pe.transpose(psH[:, c % 2, t * P:(t + 1) * P], XN[:, c * CH + t, 0:D], ident[:, :])
                        i.then_inc(xnT_psum, 1)
                    if c > 0:
                        pe.wait_ge(xnT_done, CHUNKS * l + c)
                        if c > 1:
                            pe.wait_ge(logits_out, CHUNKS * l + c - 1)
                        for t in range(CH):
                            tok = ((c - 1) * CH + t) * P
                            i = pe.matmul(psY[:, t * P:(t + 1) * P], XNT[:, tok:tok + P], GATE[:, :],
                                          start=True, stop=True)
                        i.then_inc(logits_done, 1)

                def in_shared(s):
                    f = s.u % FT
                    chunk = XNT[:, bass.ds(s.over(FT) * CH * P, CH * P)]
                    if s.past(2):
                        pe.wait_ge(silu_done, s.i + (first_shared[l] - 1))
                    pe.matmul(psG[:, s.u % 2, :], W1S[:, f * P:(f + 1) * P], chunk, start=True, stop=True)\
                      .then_inc(g_full, 1)
                    if s.past(2):
                        pe.wait_ge(h_done, s.i + (first_shared[l] - 1))
                    pe.matmul(psU[:, s.u % 2, :], W3S[:, f * P:(f + 1) * P], chunk, start=True, stop=True)\
                      .then_inc(u_full, 1)

                def out_shared(s):
                    if s.u % FT:
                        return
                    c, par = s.over(FT), s.u // FT
                    pe.wait_ge(h_done, s.i + (first_shared[l] + FT))
                    if s.past(2 * FT):
                        pe.wait_ge(sh_added, c + (CHUNKS * l - 1))
                    for t in range(CH):
                        for f in range(FT):
                            i = pe.matmul(psH[:, par, t * D:(t + 1) * D], hs[:, par, f, t * P:(t + 1) * P],
                                          W2S[:, f, :], start=(f == 0), stop=(f == FT - 1))
                    i.then_inc(sh_full, 1)

                def rank():
                    pe.wait_ge(picked, l + 1)
                    flat = chosen16[:, :, :].rearrange("p i e -> p (i e)")
                    pe.matmul(psY[:, 0:TILES * E], before[:, :], flat, start=True, stop=True)
                    pe.matmul(psY[:, TILES * E:2 * TILES * E], ones16[:, :], flat, start=True, stop=True)\
                      .then_inc(ranked, 1)

                pipelined(pe, [(in_shared, 0), (out_shared, 5)], SHARED, 2 * FT, at={2: rank})
                pe.wait_ge(w_off_done, l + 1)
                pe.wait_ge(experts_in, 48)
                pe.wait_ge(ranks_read, l + 1)
                pe.wait_ge(sh_added, CHUNKS * (l + 1))

                def transpose_rows(s):
                    if s.u % GT:
                        return
                    g, par = s.over(GT), s.u // GT
                    pe.wait_ge(rows_in[par], 16 * (s.over(2 * GT) + (l * GROUPS // 2 + 1)))
                    if s.past(2):
                        pe.wait_ge(xT_done, g + GROUPS * l)
                    for t in range(GT):
                        i = pe.transpose(psT[:, t * P:(t + 1) * P], rows[:, par, t, 0:D], ident[:, :])
                    i.then_inc(xT_psum, 1)

                def in_routed(s):
                    par = s.u // GT
                    tile = xT[:, par, s.u % GT, :]
                    at = table_entry(s.i)
                    if s.u % GT == 0:
                        pe.wait_ge(xT_done, s.over(GT) + (GROUPS * l + 1))
                    pe.wait_ge(silu_done, s.i + (first_routed[l] - 1))
                    pe.matmul(psG[:, s.u % 2, :], tile, W1[:, bass.ds(at, F)], start=True, stop=True)\
                      .then_inc(g_full, 1)
                    pe.wait_ge(h_done, s.i + (first_routed[l] - 1))
                    pe.matmul(psU[:, s.u % 2, :], tile, W3[:, bass.ds(at, F)], start=True, stop=True)\
                      .then_inc(u_full, 1)

                def transpose_h(s):
                    pe.wait_ge(h_done, s.i + (first_routed[l] + 1))
                    if s.past(2):
                        pe.wait_ge(hT_done, s.i + (TILES_R * l - 1))
                    for f in range(FT):
                        i = pe.transpose(psH[:, s.u % 2, f * P:(f + 1) * P], hr[:, s.u % 2, f * P:(f + 1) * P],
                                         ident[:, :])
                    i.then_inc(hT_psum, 1)

                def out_routed(s):
                    at = table_entry(s.i)
                    pe.wait_ge(hT_done, s.i + (TILES_R * l + 1))
                    if s.u % GT == 0 and s.past(GT):
                        pe.wait_ge(y_done, s.over(GT) + GROUPS * l)
                    t = s.u % GT
                    for f in range(FT):
                        i = pe.matmul(psY[:, t * D:(t + 1) * D], hT[:, s.u % 2, f, :],
                                      W2[:, bass.ds(at + f * D, D)], start=(f == 0), stop=(f == FT - 1))
                    i.then_inc(y_psum, 1)

                pipelined(pe, [(in_routed, 2), (transpose_h, 3), (out_routed, 4), (transpose_rows, 0)],
                          TILES_R, 2 * GT)
                if l == 1:
                    continue
                pe.wait_ge(attn_in, 48)

                def transpose_xr(s):
                    pe.wait_ge(xr_done, s.i + 1)
                    if s.past(2):
                        pe.wait_ge(xrT_done, s.i)
                    for t in range(TB):
                        i = pe.transpose(psH[:, 0, t * P:(t + 1) * P], xr[:, s.u, t, :], ident[:, :])
                    i.then_inc(xrT_psum, 1)

                def qkv(s):
                    pe.wait_ge(xrT_done, s.i + 1)
                    if s.past(1):
                        pe.wait_ge(kv_done, s.i)
                    for t in range(TB):
                        i = pe.matmul(psG[:, t, 0:3 * D], xrT[:, s.u, t * P:(t + 1) * P], WQKV[:, :],
                                      start=True, stop=True)
                    i.then_inc(qkv_psum, 1)

                def cumulate(s):
                    pe.wait_ge(kv_done, s.i + 1)
                    if s.past(1):
                        pe.wait_ge(ya_done, s.i)
                    part = [wkv[:, s.u, t, :, :].rearrange("p a d -> p (a d)") for t in range(TB)]
                    pe.matmul(psU[:, 0, 0:256], upto[:, :], part[0], start=True, stop=True)
                    pe.matmul(psU[:, 0, 256:512], ones[:, :], part[0], start=True, stop=False)
                    pe.matmul(psU[:, 0, 256:512], upto[:, :], part[1], start=False, stop=True)\
                      .then_inc(cum_psum, 1)

                def transpose_y(s):
                    pe.wait_ge(ya_done, s.i + 1)
                    if s.past(1):
                        pe.wait_ge(yT_done, s.i)
                    for t in range(TB):
                        i = pe.transpose(psH[:, 1, t * P:(t + 1) * P], ya[:, s.u, t, :], ident[:, :])
                    i.then_inc(yT_psum, 1)

                def swiglu(s):
                    pe.wait_ge(yT_done, s.i + 1)
                    if s.past(1):
                        pe.wait_ge(ha_done, s.i)
                    for a in range(2):
                        i = pe.matmul(psU[:, 1, a * 256:(a + 1) * 256], WSW[:, a * D:(a + 1) * D], yT[:, s.u, :],
                                      start=True, stop=True)
                    i.then_inc(uv_psum, 1)

                def project(s):
                    pe.wait_ge(ha_done, s.i + 1)
                    if s.past(1):
                        pe.wait_ge(at_added, s.i)
                    for t in range(TB):
                        i = pe.matmul(psT[:, t * D:(t + 1) * D], ha[:, s.u, t * P:(t + 1) * P], WOUT[:, :],
                                      start=True, stop=True)
                    i.then_inc(at_psum, 1)

                pipelined(pe, [(project, 4), (transpose_y, 3), (swiglu, 3), (cumulate, 2),
                               (transpose_xr, 0), (qkv, 0)], BATCHES, 2)


_INS = ["x", "w_qkvT", "w_swigluT", "w_outT", "gateT", "w1_e", "w3_e", "w2_e", "w1_s", "w3_s", "w2_s"]


def kernel(L0_attn_x, L0_attn_w_qkv, L0_attn_w_swiglu, L0_attn_w_out, L0_ffn_gate_W, L0_ffn_w1_e,
           L0_ffn_w3_e, L0_ffn_w2_e, L0_ffn_w1_s, L0_ffn_w3_s, L0_ffn_w2_s):
    import numpy as np
    import concourse.bacc as bacc
    from concourse.bass_utils import run_bass_kernel_spmd

    def lay(a):
        return np.ascontiguousarray(a)

    x = np.asarray(L0_attn_x)
    gateT = np.zeros((D, P), np.float32)
    gateT[:, :E] = np.asarray(L0_ffn_gate_W).T
    w1, w3, w2 = (np.asarray(a) for a in (L0_ffn_w1_e, L0_ffn_w3_e, L0_ffn_w2_e))
    arrays = {
        "x": lay(x.reshape(NT, D)),
        "w_qkvT": lay(np.asarray(L0_attn_w_qkv).T),
        "w_swigluT": lay(np.asarray(L0_attn_w_swiglu).T),
        "w_outT": lay(np.asarray(L0_attn_w_out).T),
        "gateT": gateT,
        "w1_e": lay(w1.transpose(1, 0, 2).reshape(D, E * F)),
        "w3_e": lay(w3.transpose(1, 0, 2).reshape(D, E * F)),
        "w2_e": lay(w2.reshape(E, FT, P, D).transpose(2, 0, 1, 3).reshape(P, E * FT * D)),
        "w1_s": lay(np.asarray(L0_ffn_w1_s).transpose(1, 0, 2).reshape(D, F)),
        "w3_s": lay(np.asarray(L0_ffn_w3_s).transpose(1, 0, 2).reshape(D, F)),
        "w2_s": lay(np.asarray(L0_ffn_w2_s).reshape(F, D)),
    }
    nc = bacc.Bacc("TRN2", target_bir_lowering=False, num_devices=1)
    args = [nc.dram_tensor(n, list(arrays[n].shape), fp32, kind="ExternalInput").ap() for n in _INS]
    out = nc.dram_tensor("out", [NT, D], fp32, kind="ExternalOutput").ap()
    macaron(nc, *args, out)
    result = run_bass_kernel_spmd(nc, [arrays], core_ids=[0]).results[0]
    return result["out"].reshape(x.shape)
```

```python
import concourse.bass as bass
from concourse import mybir
from contextlib import ExitStack

P = 128
D = 128
NT = 4096
TILES = NT // P
E = 8
TOPK = 2
F = 512
FT = F // P
CH = 4
CHUNKS = TILES // CH
SEQ = 256
BATCHES = NT // SEQ
TB = SEQ // P
TILES_R = TOPK * NT // P + E
GT = 4
GROUPS = TILES_R // GT
ROW = D + 2
LN_EPS = 1e-5
RMS_EPS = 1.1920929e-07
NS = 8

POOL_STAGES = [("at_rsqrt", 2), ("qkv_rsqrt", 4), ("residual", 4), ("add_routed", 0)]
DVE_STAGES = [("gate_u", 7), ("at_statistics", 1), ("attend", 5), ("weigh_v", 4), ("at_normalise", 2),
              ("add_attention", 8)]
ACT_STAGES = [("denominator", 5), ("copy_anT", 3), ("weights", 4), ("tanh_g", 6), ("copy_yT", 5),
              ("squares", 3)]
PE_STAGES = [("project", 8), ("swiglu", 6), ("qkv", 3), ("transpose_y", 5), ("cumulate", 4),
             ("transpose_xn", 2)]

fp32 = mybir.dt.float32
bf16 = mybir.dt.bfloat16
i32 = mybir.dt.int32
ALU = mybir.AluOpType
ACT = mybir.ActivationFunctionType
X_AXIS = mybir.AxisListType.X


class Step:

    def __init__(self, r, u, unroll, first):
        self.r, self.u, self.unroll, self.first = r, u, unroll, first
        self.i = r * unroll + u

    def past(self, n):
        return self.first >= n or not isinstance(self.r, int)

    def over(self, n):
        return self.r * (self.unroll // n) + self.u // n


def pipelined(eng, stages, count, unroll, guard=2, at=None):
    deepest = max(d for _, d in stages)
    head = -(-(deepest + guard) // unroll) * unroll

    def static(k):
        if at and k in at:
            at[k]()
        for stage, d in stages:
            i = k - d
            if 0 <= i < count:
                stage(Step(i // unroll, i % unroll, unroll, i))

    for k in range(min(head, count)):
        static(k)
    if count > head:
        with eng.Fori(0, (count - head) // unroll) as r:
            for u in range(unroll):
                for stage, d in stages:
                    k = head + u - d
                    stage(Step(r + k // unroll, k % unroll, unroll, k))
    for k in range(count, count + deepest):
        static(k)


class Chain:

    def __init__(self, eng, sem):
        self.eng, self.sem, self.n = eng, sem, 0

    def then(self, instruction):
        instruction.then_inc(self.sem, 1)
        self.n += 1
        self.eng.wait_ge(self.sem, self.n)


def macaron(nc, x, w_qkvT, w_swigluT, w_outT, gateT, w1_e, w3_e, w2_e, w1_s, w3_s, w2_s, out):
    ctx = ExitStack()
    with ctx:
        def sb(name, shape, dt=fp32):
            return ctx.enter_context(nc.sbuf_tensor(name, shape, dt))

        def ps(name, shape, dt=fp32):
            return ctx.enter_context(nc.psum_tensor(name, shape, dt))

        def sem(name):
            return ctx.enter_context(nc.semaphore(name))

        slots = [nc.dram_tensor(f"slots{l}", [TILES_R * P, ROW], fp32, kind="Internal").ap() for l in range(2)]
        results = nc.dram_tensor("results", [(TOPK * TILES + TILES_R) * P, D], fp32, kind="Internal").ap()

        X = sb("X", [P, TILES, D])
        XN = sb("XN", [P, TILES, ROW])
        XNT = sb("XNT", [P, NT])
        W1 = sb("W1", [P, E * F])
        W3 = sb("W3", [P, E * F])
        W2 = sb("W2", [P, E * FT * D])
        W1S = sb("W1S", [P, F])
        W3S = sb("W3S", [P, F])
        W2S = sb("W2S", [P, FT, D])
        GATE = sb("GATE", [P, P])
        WQKV = sb("WQKV", [P, 3 * D])
        WSW = sb("WSW", [P, 2 * D])
        WOUT = sb("WOUT", [P, D])
        ident = sb("ident", [P, P])
        ones = sb("ones", [P, P])
        upto = sb("upto", [P, P])
        before = sb("before", [P, P], bf16)
        ones16 = sb("ones16", [P, P], bf16)
        rev_e = sb("rev_e", [P, E])
        tile_starts = sb("tile_starts", [P, TILES])
        tile_no = sb("tile_no", [P, TILES_R])
        slot_no = sb("slot_no", [P, TILES_R])
        targets = sb("targets", [P, TOPK, TILES], i32)
        pad_rows = sb("pad_rows", [P, ROW])
        minus_half = sb("minus_half", [P, 3 * TB])
        one_row = sb("one_row", [P, E * TILES])
        ln_stats = sb("ln_stats", [P, 2, CH, 6])
        ln_mv = sb("ln_mv", [P, 2, CH, 2])
        ln_var = sb("ln_var", [P, 2, CH])
        ln_rstd = sb("ln_rstd", [P, 2, CH])
        logit = sb("logit", [P, TILES, E])
        prob = sb("prob", [P, TILES, E])
        cand = sb("cand", [P, TILES, E])
        onehot = [sb(f"onehot{k}", [P, TILES, E]) for k in range(TOPK)]
        chosen16 = sb("chosen16", [P, TILES, E], bf16)
        row_a = sb("row_a", [P, TILES])
        row_b = sb("row_b", [P, TILES])
        top = [sb(f"top{k}", [P, TILES]) for k in range(TOPK)]
        tot = sb("tot", [P, E, TILES])
        cum = sb("cum", [P, E, TILES])
        excl = sb("excl", [P, E, TILES])
        pick = sb("pick", [P, E, TILES])
        cnt = sb("cnt", [P, E])
        need = sb("need", [P, E, TILES])
        ntile = sb("ntile", [P, E])
        tend = sb("tend", [P, E])
        tstart = sb("tstart", [P, E])
        shift = sb("shift", [P, E])
        tile_cmp = sb("tile_cmp", [P, TILES_R, E])
        tile_e = sb("tile_e", [P, TILES_R])
        w_off = sb("w_off", [P, TILES_R], i32)
        posf = sb("posf", [P, TILES])
        pos = [sb(f"pos{k}", [P, TILES], i32) for k in range(TOPK)]
        silu = sb("silu", [P, 2, F])
        hs = sb("hs", [P, 2, FT, CH * P])
        rows = sb("rows", [P, 2, GT, ROW])
        xT = sb("xT", [P, 2, GT, P])
        tile_gate = sb("tile_gate", [P, 2, GT])
        own_row = sb("own_row", [P, 2, GT])
        tile_tgt = sb("tile_tgt", [P, 2, GT], i32)
        hr = sb("hr", [P, 2, F])
        hT = sb("hT", [P, 2, FT, P])
        yout = sb("yout", [P, 2, GT, D])
        ytgt = sb("ytgt", [P, 2, GT], i32)
        Y = sb("Y", [P, 4, TOPK, TB, D])
        at_stats = sb("at_stats", [P, 2, TB, 6])
        at_mv = sb("at_mv", [P, 2, TB, 2])
        at_var = sb("at_var", [P, 2, 2, TB])
        at_rstd = sb("at_rstd", [P, 2, TB])
        at_sq = sb("at_sq", [P, 2, TB])
        at_eps = sb("at_eps", [P, 2, 2, TB])
        at_ms = sb("at_ms", [P, 2, 3, TB])
        at_fac = sb("at_fac", [P, 2, 3, TB])
        xn = sb("xn", [P, 2, TB, D])
        anT = sb("anT", [P, 2, TB * P])
        sq = sb("sq", [P, 2, TB, D], bf16)
        qk_ss = sb("qk_ss", [P, 2, 2, TB])
        wkv = sb("wkv", [P, 2, TB, 2, D])
        tq = sb("tq", [P, 2, TB, D])
        den = sb("den", [P, 2, TB, D])
        rec = sb("rec", [P, 2, TB, D])
        ysc = sb("ysc", [P, 2, TB, D])
        ya = sb("ya", [P, 2, TB, D])
        yT = sb("yT", [P, 2, TB * P])
        tg = sb("tg", [P, 2, TB * P])
        ag = sb("ag", [P, 2, TB * P])
        ha = sb("ha", [P, 2, TB * P])

        psG = ps("psG", [P, 2, 512])
        psU = ps("psU", [P, 2, 512])
        psH = ps("psH", [P, 2, 512])
        psT = ps("psT", [P, 512])
        psY = ps("psY", [P, 512])

        x_in = [sem(f"x_in{c}") for c in range(CHUNKS)]
        small_in = sem("small_in")
        experts_in = sem("experts_in")
        attn_in = sem("attn_in")
        padded = [sem(f"padded{l}") for l in range(2)]
        consts = sem("consts")
        const_link = sem("const_link")
        ln_link = sem("ln_link")
        ln_stat = sem("ln_stat")
        ln_scaled = sem("ln_scaled")
        xn_done = sem("xn_done")
        xnT_psum = sem("xnT_psum")
        xnT_done = sem("xnT_done")
        logits_done = sem("logits_done")
        logits_out = sem("logits_out")
        route_link = sem("route_link")
        shifted = sem("shifted")
        expd = sem("expd")
        picked = sem("picked")
        ranked = sem("ranked")
        ranks_read = sem("ranks_read")
        w_off_done = sem("w_off_done")
        pos_done = sem("pos_done")
        sent = [sem(f"sent{k}") for k in range(TOPK)]
        retarget = sem("retarget")
        g_full = sem("g_full")
        u_full = sem("u_full")
        silu_done = sem("silu_done")
        h_done = sem("h_done")
        sh_full = sem("sh_full")
        sh_added = sem("sh_added")
        rows_in = [sem(f"rows_in{p}") for p in range(2)]
        xT_psum = sem("xT_psum")
        xT_done = sem("xT_done")
        tgt_link = sem("tgt_link")
        hT_psum = sem("hT_psum")
        hT_done = sem("hT_done")
        y_psum = sem("y_psum")
        y_done = sem("y_done")
        y_sent = [sem(f"y_sent{p}") for p in range(2)]
        y_in = [sem(f"y_in{p}") for p in range(4)]
        add_link = sem("add_link")
        routed_added = sem("routed_added")
        half_added = sem("half_added")
        out_sent = sem("out_sent")
        at_link = sem("at_link")
        at_stat = sem("at_stat")
        sq_link = sem("sq_link")
        rms_terms = sem("rms_terms")
        at_scaled = sem("at_scaled")
        xn_ready = sem("xn_ready")
        xres_done = sem("xres_done")
        anT_psum = sem("anT_psum")
        anT_done = sem("anT_done")
        qkv_psum = sem("qkv_psum")
        ss_done = sem("ss_done")
        qk_scaled = sem("qk_scaled")
        w_done = sem("w_done")
        qk_link = sem("qk_link")
        kv_done = sem("kv_done")
        cum_psum = sem("cum_psum")
        den_done = sem("den_done")
        y_link = sem("y_link")
        ya_done = sem("ya_done")
        yT_psum = sem("yT_psum")
        yT_done = sem("yT_done")
        uv_psum = sem("uv_psum")
        tg_done = sem("tg_done")
        h_link = sem("h_link")
        ha_done = sem("ha_done")
        at_psum = sem("at_psum")
        at_added = sem("at_added")

        psQKV = [psG, psH]

        block = ctx.enter_context(nc.Block())
        CONSTS = 13
        SHARED = CHUNKS * FT
        first_shared = [l * (SHARED + TILES_R) for l in range(2)]
        first_routed = [f + SHARED for f in first_shared]

        def wait_apart(eng, semaphore, value):
            if isinstance(value, int):
                eng.wait_ge(semaphore, value)
                return
            with eng.register() as wanted:
                eng.reg_mov(wanted, value)
                eng.wait_ge(consts, CONSTS)
                eng.wait_ge(semaphore, wanted)

        x_v = x.rearrange("(i p) d -> p i d", p=P)
        out_v = out.rearrange("(i p) d -> p i d", p=P)
        results_v = results[0:TOPK * NT, :].rearrange("(k i p) d -> p k i d", k=TOPK, p=P)

        @block.sync
        def _(sp):
            for c in range(CHUNKS):
                sp.dma_start(X[:, c * CH:(c + 1) * CH, :], x_v[:, c * CH:(c + 1) * CH, :]).then_inc(x_in[c], 16)
                if c == 1:
                    for dst, src in ((GATE[:, :], gateT), (W1S[:, :], w1_s), (W3S[:, :], w3_s),
                                     (W2S[:, :, :], w2_s.rearrange("(j p) d -> p j d", p=P))):
                        sp.dma_start(dst, src).then_inc(small_in, 16)
            sp.wait_ge(consts, CONSTS)
            for l in range(2):
                if l == 1:
                    for dst, src in ((W1[:, :], w1_e), (W3[:, :], w3_e),
                                     (W2[:, :], w2_e)):
                        sp.dma_start(dst, src).then_inc(experts_in, 16)
                    for dst, src in ((WQKV[:, :], w_qkvT), (WSW[:, :], w_swigluT), (WOUT[:, :], w_outT)):
                        sp.dma_start(dst, src).then_inc(attn_in, 16)
                sp.dma_start(slots[l].rearrange("(j p) c -> p j c", p=P),
                             pad_rows[:, :].unsqueeze(1).to_broadcast([P, TILES_R, ROW])).then_inc(padded[l], 16)
            for l in range(2):
                slots_v = slots[l].rearrange("(g t p) c -> g p t c", t=GT, p=P)
                for k in range(TOPK):
                    sp.wait_ge(sent[k], 16 * TILES * (l + 1))

                def load_rows(s):
                    if s.past(2):
                        sp.wait_ge(xT_done, s.i + (l * GROUPS - 1))
                    sp.dma_start(rows[:, s.u, :, :], slots_v[bass.ds(s.i, 1), :, :, :].squeeze(0)
                                 if not isinstance(s.i, int) else slots_v[s.i, :, :, :]).then_inc(rows_in[s.u], 16)

                pipelined(sp, [(load_rows, 0)], GROUPS, 2)
                for p in range(2):
                    sp.wait_ge(y_sent[p], 16 * TILES_R // 2 * (l + 1))

                def load_results(s):
                    if s.past(4):
                        sp.wait_ge(routed_added, s.i + (l * BATCHES - 3))
                    for k in range(TOPK):
                        sp.dma_start(Y[:, s.u, k, :, :], results_v[:, k, bass.ds(s.i * TB, TB), :])\
                          .then_inc(y_in[s.u], 16)

                pipelined(sp, [(load_results, 0)], BATCHES, 4)

        @block.gpsimd
        def _(pool):
            one = Chain(pool, const_link)
            pool.memset(ones[:, :], 1.0).then_inc(consts, 1)
            pool.memset(ones16[:, :], 1.0).then_inc(consts, 1)
            pool.memset(minus_half[:, :], -0.5).then_inc(consts, 1)
            pool.memset(one_row[:, :], 1.0).then_inc(consts, 1)
            one.then(pool.memset(ident[:, :], 0.0))
            one.then(pool.memset(upto[:, :], 1.0))
            one.then(pool.memset(before[:, :], 1.0))
            one.then(pool.memset(pad_rows[:, :], 0.0))
            pool.affine_select(out=ident[:, :], in_=ident[:, :], compare_op=ALU.not_equal, fill=1.0,
                               base=0, pattern=[[-1, P]], channel_multiplier=1).then_inc(consts, 1)
            pool.affine_select(out=upto[:, :], in_=upto[:, :], compare_op=ALU.is_ge, fill=0.0,
                               base=0, pattern=[[1, P]], channel_multiplier=-1).then_inc(consts, 1)
            pool.affine_select(out=before[:, :], in_=before[:, :], compare_op=ALU.is_gt, fill=0.0,
                               base=0, pattern=[[1, P]], channel_multiplier=-1).then_inc(consts, 1)
            pool.iota(slot_no[:, :], pattern=[[P, TILES_R]], base=0, channel_multiplier=1,
                      allow_small_or_imprecise_dtypes=True).then_inc(consts, 1)
            pool.iota(pad_rows[:, D + 1:D + 2].bitcast(i32), pattern=[[0, 1]], base=TOPK * NT,
                      channel_multiplier=0).then_inc(consts, 1)
            pool.iota(rev_e[:, :], pattern=[[-1, E]], base=E, channel_multiplier=0,
                      allow_small_or_imprecise_dtypes=True).then_inc(consts, 1)
            pool.iota(tile_starts[:, :], pattern=[[P, TILES]], base=0, channel_multiplier=0,
                      allow_small_or_imprecise_dtypes=True).then_inc(consts, 1)
            pool.iota(tile_no[:, :], pattern=[[1, TILES_R]], base=0, channel_multiplier=0,
                      allow_small_or_imprecise_dtypes=True).then_inc(consts, 1)
            pool.iota(targets[:, :, :], pattern=[[NT, TOPK], [P, TILES]], base=0,
                      channel_multiplier=1).then_inc(consts, 1)
            pool.wait_ge(consts, CONSTS)

            def add_routed(s):
                    xs = X[:, bass.ds(s.i * TB, TB), :]
                    wait_apart(pool, y_in[s.u % 4], 16 * TOPK * (s.over(4) + 1))
                    if s.first == 0:
                        pool.wait_ge(sh_added, CHUNKS)
                    pool.tensor_tensor(xs, xs, Y[:, s.u % 4, 0, :, :], ALU.add).then_inc(add_link, 1)
                    wait_apart(pool, add_link, s.i + 1)
                    pool.tensor_tensor(xs, xs, Y[:, s.u % 4, 1, :, :], ALU.add).then_inc(routed_added, 1)

            for l in range(2):
                def scale_ln(s):
                    pool.wait_ge(ln_stat, s.i + (l * CHUNKS + 1))
                    pool.tensor_tensor(ln_rstd[:, s.u, :], ln_var[:, s.u, :], minus_half[:, 0:CH], ALU.pow)\
                        .then_inc(ln_scaled, 1)

                pipelined(pool, [(scale_ln, 0)], CHUNKS, 2)
                pool.wait_ge(padded[l], 16)
                for k in range(TOPK):
                    pool.wait_ge(pos_done, TOPK * l + k + 1)
                    if k == 1:
                        pool.wait_ge(sent[0], 16 * TILES * (l + 1))
                        pool.tensor_scalar(XN[:, :, D], top[1][:, :], 0.25, None, ALU.mult).then_inc(retarget, 1)
                        pool.tensor_copy(XN[:, :, D + 1].bitcast(i32), targets[:, 1, :]).then_inc(retarget, 1)
                        pool.wait_ge(retarget, 2 * (l + 1))
                    for i in range(TILES):
                        pool.indirect_dma_start(slots[l], bass.IndirectOffsetOnAxis(ap=pos[k][:, i:i + 1], axis=0),
                                                XN[:, i, :], None).then_inc(sent[k], 16)

                def send_results(s):
                    wait_apart(pool, y_done, s.i + (l * GROUPS + 1))
                    for t in range(GT):
                        pool.indirect_dma_start(
                            results, bass.IndirectOffsetOnAxis(ap=ytgt[:, s.u, t:t + 1], axis=0),
                            yout[:, s.u, t, :], None).then_inc(y_sent[s.u], 16)

                pipelined(pool, [(send_results, 0)], GROUPS, 2)

                def at_rsqrt(s):
                    pool.wait_ge(at_stat, s.i + 1)
                    pool.tensor_tensor(at_rstd[:, s.u % 2, :], at_var[:, s.u % 2, 0, :], minus_half[:, 0:TB], ALU.pow)\
                        .then_inc(at_scaled, 1)

                def residual(s):
                    wait_apart(pool, xn_ready, s.i + 1)
                    xs = X[:, bass.ds(s.i * TB, TB), :]
                    pool.tensor_tensor(xs, xs, xn[:, s.u % 2, :, :], ALU.add).then_inc(xres_done, 1)

                def qkv_rsqrt(s):
                    pool.wait_ge(ss_done, s.i + 1)
                    pool.wait_ge(rms_terms, s.i + 1)
                    if s.past(2):
                        pool.wait_ge(kv_done, s.i - 1)
                    ms = at_ms[:, s.u % 2, :, :]
                    pool.tensor_tensor(ms[:, 0:2, :], qk_ss[:, s.u % 2, :, :], at_eps[:, s.u % 2, :, :], ALU.add)\
                        .then_inc(qk_link, 1)
                    pool.wait_ge(qk_link, s.i + 1)
                    pool.tensor_tensor(at_fac[:, s.u % 2, :, :], ms, minus_half[:, 0:3 * TB]
                                       .rearrange("p (a t) -> p a t", a=3), ALU.pow).then_inc(qk_scaled, 1)

                if l == 0:
                    stages = {"qkv_rsqrt": qkv_rsqrt, "add_routed": add_routed, "residual": residual,
                              "at_rsqrt": at_rsqrt}
                    pipelined(pool, [(stages[n], d) for n, d in POOL_STAGES], BATCHES, 4)

        @block.vector
        def _(dve):
            dve.wait_ge(consts, CONSTS)
            route = Chain(dve, route_link)

            def wide(ap, shape):
                return ap.unsqueeze(2).to_broadcast(shape)

            TE = [P, TILES, E]
            ET = [P, E, TILES]
            for l in range(2):
                def stats(s):
                    if l == 0:
                        dve.wait_ge(x_in[s.i], 16)
                    elif s.first == 0:
                        dve.wait_ge(at_added, BATCHES)
                    base = 2 * CHUNKS * l
                    for t in range(CH):
                        i = dve.bn_stats(ln_stats[:, s.u % 2, t, :], X[:, s.i * CH + t, :])
                    i.then_inc(ln_link, 1)
                    dve.wait_ge(ln_link, base + 2 * s.i + 1)
                    for t in range(CH):
                        i = dve.bn_aggr(ln_mv[:, s.u % 2, t, :], ln_stats[:, s.u % 2, t, :])
                    i.then_inc(ln_link, 1)
                    dve.wait_ge(ln_link, base + 2 * s.i + 2)
                    dve.tensor_scalar(ln_var[:, s.u % 2, :], ln_mv[:, s.u % 2, :, 1], LN_EPS, None, ALU.add)\
                       .then_inc(ln_stat, 1)

                def normalise(s):
                    dve.wait_ge(ln_scaled, s.i + (l * CHUNKS + 1))
                    for t in range(CH):
                        i = dve.tensor_scalar(XN[:, s.i * CH + t, 0:D], X[:, s.i * CH + t, :],
                                              ln_mv[:, s.u % 2, t, 0:1], ln_rstd[:, s.u % 2, t:t + 1],
                                              ALU.subtract, ALU.mult)
                    i.then_inc(xn_done, 1)

                for c in range(CHUNKS + 1):
                    if c < CHUNKS:
                        stats(Step(c // 2, c % 2, 2, c))
                    if c > 0:
                        normalise(Step((c - 1) // 2, (c - 1) % 2, 2, c - 1))

                def gated(hidden, s, base):
                    dve.wait_ge(silu_done, s.i + (base + 1))
                    dve.wait_ge(u_full, s.i + (base + 1))
                    dve.tensor_tensor(hidden, silu[:, s.u % 2, :], psU[:, s.u % 2, :], ALU.mult).then_inc(h_done, 1)

                def gated_shared(s):
                    if s.past(2 * FT) and s.u % FT == 0:
                        dve.wait_ge(sh_full, s.over(FT) + (CHUNKS * l - 1))
                    gated(hs[:, s.u // FT, s.u % FT, :], s, first_shared[l])

                done = [0]

                def shared_steps(n):
                    for _ in range(n):
                        gated_shared(Step(0, done[0], 2 * FT, done[0]))
                        done[0] += 1

                dve.wait_ge(logits_out, CHUNKS * (l + 1))
                route.then(dve.tensor_reduce(row_a[:, :], logit[:, :, :], X_AXIS, ALU.max))
                dve.tensor_tensor(cand[:, :, :], logit[:, :, :], wide(row_a[:, :], TE), ALU.subtract)\
                   .then_inc(shifted, 1)
                dve.wait_ge(expd, l + 1)
                route.then(dve.tensor_reduce(row_b[:, :], prob[:, :, :], X_AXIS, ALU.add))
                route.then(dve.reciprocal(row_a[:, :], row_b[:, :]))
                route.then(dve.tensor_tensor(prob[:, :, :], prob[:, :, :], wide(row_a[:, :], TE), ALU.mult))
                for k in range(TOPK):
                    route.then(dve.tensor_reduce(top[k][:, :], prob[:, :, :], X_AXIS, ALU.max))
                    route.then(dve.tensor_tensor(cand[:, :, :], prob[:, :, :], wide(top[k][:, :], TE), ALU.is_ge))
                    route.then(dve.tensor_tensor(cand[:, :, :], cand[:, :, :],
                                                 rev_e[:, :].unsqueeze(1).to_broadcast(TE), ALU.mult))
                    route.then(dve.tensor_reduce(row_b[:, :], cand[:, :, :], X_AXIS, ALU.max))
                    route.then(dve.tensor_tensor(onehot[k][:, :, :], rev_e[:, :].unsqueeze(1).to_broadcast(TE),
                                                 wide(row_b[:, :], TE), ALU.is_equal))
                    shared_steps(1 + k)
                    if k == 0:
                        route.then(dve.scalar_tensor_tensor(prob[:, :, :], onehot[0][:, :, :], -2.0,
                                                            prob[:, :, :], ALU.mult, ALU.add))
                dve.tensor_tensor(chosen16[:, :, :], onehot[0][:, :, :], onehot[1][:, :, :], ALU.add)\
                   .then_inc(picked, 1)

                def slots_of():
                    dve.wait_ge(ranked, l + 1)
                    within = psY[:, 0:TILES * E].rearrange("p (i e) -> p e i", e=E)
                    totals = psY[:, TILES * E:2 * TILES * E].rearrange("p (i e) -> p e i", e=E)
                    route.then(dve.tensor_copy(tot[:, :, :], totals))
                    flat = "p e i -> p (e i)"
                    route.then(dve.tensor_tensor_scan(cum[:, :, :].rearrange(flat), one_row[:, :],
                                                      tot[:, :, :].rearrange(flat), 0.0, ALU.mult, ALU.add))
                    route.then(dve.tensor_tensor(excl[:, :, :], cum[:, :, :], tot[:, :, :], ALU.subtract))
                    route.then(dve.tensor_tensor(cnt[:, :], cum[:, :, TILES - 1], excl[:, :, 0], ALU.subtract))
                    shared_steps(1)
                    route.then(dve.tensor_tensor(need[:, :, :], wide(cnt[:, :], ET),
                                                 tile_starts[:, :].unsqueeze(1).to_broadcast(ET), ALU.is_gt))
                    route.then(dve.tensor_reduce(ntile[:, :], need[:, :, :], X_AXIS, ALU.add))
                    route.then(dve.tensor_tensor_scan(tend[:, :], one_row[:, 0:E], ntile[:, :], 0.0,
                                                      ALU.mult, ALU.add))
                    route.then(dve.tensor_tensor(tstart[:, :], tend[:, :], ntile[:, :], ALU.subtract))
                    route.then(dve.scalar_tensor_tensor(shift[:, :], tstart[:, :], float(P), excl[:, :, 0],
                                                        ALU.mult, ALU.subtract))
                    route.then(dve.tensor_tensor(excl[:, :, :], excl[:, :, :], wide(shift[:, :], ET), ALU.add))
                    i = dve.tensor_tensor(excl[:, :, :], excl[:, :, :], within, ALU.add)
                    i.then_inc(ranks_read, 1)
                    dve.wait_ge(ranks_read, l + 1)
                    for k in range(TOPK):
                        route.then(dve.tensor_tensor(pick[:, :, :], excl[:, :, :],
                                                     onehot[k][:, :, :].rearrange("p i e -> p e i"), ALU.mult))
                        route.then(dve.tensor_reduce(posf[:, :], pick[:, :, :].rearrange("p e i -> p i e"),
                                                     X_AXIS, ALU.add))
                        i = dve.tensor_copy(pos[k][:, :], posf[:, :])
                        if k == 0:
                            route.then(i)
                            route.then(dve.tensor_scalar(XN[:, :, D], top[0][:, :], 0.25, None, ALU.mult))
                            i = dve.tensor_copy(XN[:, :, D + 1].bitcast(i32), targets[:, 0, :])
                        i.then_inc(pos_done, 1)
                        shared_steps(2)
                        if k == 0:
                            cmp3 = [P, TILES_R, E]
                            route.then(dve.tensor_tensor(tile_cmp[:, :, :], wide(tile_no[:, :], cmp3),
                                                         tend[:, :].unsqueeze(1).to_broadcast(cmp3), ALU.is_ge))
                            route.then(dve.tensor_reduce(tile_e[:, :], tile_cmp[:, :, :], X_AXIS, ALU.add))
                            dve.tensor_scalar(w_off[:, :], tile_e[:, :], float(E - 1), float(F),
                                              ALU.min, ALU.mult).then_inc(w_off_done, 1)

                def add_shared(s):
                    if s.u % FT:
                        return
                    c = s.over(FT)
                    dve.wait_ge(sh_full, c + (CHUNKS * l + 1))
                    xs = X[:, bass.ds(c * CH, CH), :].rearrange("p t d -> p (t d)")
                    dve.scalar_tensor_tensor(xs, psH[:, s.u // FT, :], 0.25 / NS, xs, ALU.mult, ALU.add)\
                       .then_inc(sh_added, 1)

                slots_of()

                def gated_rest(s):
                    if s.past(done[0]):
                        gated_shared(s)

                pipelined(dve, [(gated_rest, 0), (add_shared, 6)], SHARED, 2 * FT)

                def gated_routed(s):
                    if s.past(2):
                        dve.wait_ge(hT_psum, s.i + (TILES_R * l - 1))
                    gated(hr[:, s.u % 2, :], s, first_routed[l])

                def copy_xT(s):
                    if s.u % GT:
                        return
                    g, par = s.over(GT), s.u // GT
                    dve.wait_ge(xT_psum, g + (GROUPS * l + 1))
                    if s.past(2 * GT):
                        dve.wait_ge(u_full, s.i + (first_routed[l] - GT))
                    dve.tensor_copy(xT[:, par, :, :].rearrange("p t c -> p (t c)"), psT[:, :])
                    dve.tensor_copy(tile_gate[:, par, :], rows[:, par, :, D])
                    target = rows[:, par, :, D + 1].bitcast(i32)
                    dve.scalar_tensor_tensor(own_row[:, par, :], target, float(TOPK * NT), slot_no[:, bass.ds(s.i, GT)],
                                             ALU.is_ge, ALU.mult).then_inc(tgt_link, 1)
                    dve.wait_ge(tgt_link, g + (GROUPS * l + 1))
                    dve.tensor_tensor(tile_tgt[:, par, :], own_row[:, par, :], target, ALU.add).then_inc(xT_done, 1)

                def scale_y(s):
                    if s.u % GT != GT - 1:
                        return
                    g, par = s.over(GT), s.u // GT
                    dve.wait_ge(y_psum, s.i + (TILES_R * l + 1))
                    dve.wait_ge(xT_done, g + (GROUPS * l + 1))
                    if s.past(2 * GT):
                        dve.wait_ge(y_sent[par], 16 * GT * (s.over(2 * GT) + l * GROUPS // 2))
                    for t in range(GT):
                        dve.tensor_scalar(yout[:, par, t, :], psY[:, t * D:(t + 1) * D],
                                          tile_gate[:, par, t:t + 1], None, ALU.mult)
                    dve.tensor_copy(ytgt[:, par, :], tile_tgt[:, par, :]).then_inc(y_done, 1)

                pipelined(dve, [(gated_routed, 2), (scale_y, 4), (copy_xT, 0)], TILES_R, 2 * GT)

                if l == 1:
                    continue

                def at_statistics(s):
                    dve.wait_ge(routed_added, s.i + 1)
                    for t in range(TB):
                        i = dve.bn_stats(at_stats[:, s.u, t, :],
                                         X[:, bass.ds(s.i * TB + t, 1), :].rearrange("p a d -> p (a d)"))
                    i.then_inc(at_link, 1)
                    wait_apart(dve, at_link, s.i * 2 + 1)
                    for t in range(TB):
                        i = dve.bn_aggr(at_mv[:, s.u, t, :], at_stats[:, s.u, t, :])
                    i.then_inc(at_link, 1)
                    dve.wait_ge(at_link, s.i * 2 + 2)
                    dve.tensor_scalar(at_var[:, s.u, 1, :], at_mv[:, s.u, :, 1], 1.0 + RMS_EPS, RMS_EPS * LN_EPS,
                                      ALU.mult, ALU.add)
                    dve.tensor_scalar(at_var[:, s.u, 0, :], at_mv[:, s.u, :, 1], LN_EPS, None, ALU.add)\
                       .then_inc(at_stat, 1)

                def at_normalise(s):
                    dve.wait_ge(at_scaled, s.i + 1)
                    if s.past(2):
                        dve.wait_ge(anT_psum, s.i - 1)
                        dve.wait_ge(xres_done, s.i - 1)
                    for t in range(TB):
                        xt = X[:, bass.ds(s.i * TB + t, 1), :].rearrange("p a d -> p (a d)")
                        i = dve.tensor_scalar(xn[:, s.u, t, :], xt, at_mv[:, s.u, t, 0:1],
                                              at_rstd[:, s.u, t:t + 1], ALU.subtract, ALU.mult)
                    i.then_inc(xn_ready, 1)
                    dve.tensor_tensor(at_sq[:, s.u, :], at_rstd[:, s.u, :], at_rstd[:, s.u, :], ALU.mult)\
                       .then_inc(sq_link, 1)
                    dve.wait_ge(sq_link, s.i * 2 + 1)
                    if s.past(2):
                        dve.wait_ge(qk_scaled, s.i - 1)
                    dve.tensor_tensor(at_ms[:, s.u, 2, :], at_sq[:, s.u, :], at_var[:, s.u, 1, :], ALU.mult)\
                       .then_inc(sq_link, 1)
                    dve.wait_ge(sq_link, s.i * 2 + 2)
                    dve.tensor_scalar(at_eps[:, s.u, 0, :], at_ms[:, s.u, 2, :], 4 * RMS_EPS, None, ALU.mult)
                    dve.tensor_scalar(at_eps[:, s.u, 1, :], at_ms[:, s.u, 2, :], RMS_EPS, None, ALU.mult)\
                       .then_inc(rms_terms, 1)

                def weigh_v(s):
                    dve.wait_ge(w_done, s.i + 1)
                    for t in range(TB):
                        i = dve.scalar_tensor_tensor(wkv[:, s.u, t, 1, :], psQKV[s.u][:, t, 2 * D:3 * D],
                                                     at_fac[:, s.u, 2, t:t + 1], wkv[:, s.u, t, 0, :],
                                                     ALU.mult, ALU.mult)
                    i.then_inc(kv_done, 1)

                def attend(s):
                    dve.wait_ge(den_done, s.i + 1)
                    sums = psU[:, 0, :].rearrange("p (t a d) -> p t a d", t=TB, a=2)
                    dve.reciprocal(rec[:, s.u, :, :], den[:, s.u, :, :]).then_inc(y_link, 1)
                    dve.wait_ge(y_link, s.i * 2 + 1)
                    dve.scalar_tensor_tensor(ysc[:, s.u, :, :], tq[:, s.u, :, :], 1.0, rec[:, s.u, :, :],
                                             ALU.add, ALU.mult).then_inc(y_link, 1)
                    dve.wait_ge(y_link, s.i * 2 + 2)
                    if s.past(2):
                        dve.wait_ge(yT_psum, s.i - 1)
                    dve.tensor_tensor(ya[:, s.u, :, :], ysc[:, s.u, :, :], sums[:, :, 1, :], ALU.mult)\
                       .then_inc(ya_done, 1)

                def gate_u(s):
                    dve.wait_ge(tg_done, s.i + 1)
                    dve.scalar_tensor_tensor(ag[:, s.u, :], tg[:, s.u, :], 1.0, psU[:, 1, 256:512],
                                             ALU.add, ALU.mult).then_inc(h_link, 1)
                    dve.wait_ge(h_link, s.i + 1)
                    if s.past(2):
                        dve.wait_ge(at_psum, s.i - 1)
                    dve.tensor_tensor(ha[:, s.u, :], ag[:, s.u, :], psU[:, 1, 0:256], ALU.mult)\
                       .then_inc(ha_done, 1)

                def add_attention(s):
                    dve.wait_ge(at_psum, s.i + 1)
                    dve.wait_ge(xres_done, s.i + 1)
                    xs = X[:, bass.ds(s.i * TB, TB), :].rearrange("p t d -> p (t d)")
                    dve.scalar_tensor_tensor(xs, psY[:, 0:TB * D], 0.5, xs, ALU.mult, ALU.add)\
                       .then_inc(at_added, 1)

                stages = {"weigh_v": weigh_v, "gate_u": gate_u, "add_attention": add_attention,
                          "at_normalise": at_normalise, "at_statistics": at_statistics, "attend": attend}
                pipelined(dve, [(stages[n], d) for n, d in DVE_STAGES], BATCHES, 2)

            def add_last(s):
                xs = X[:, bass.ds(s.i * TB, TB), :]
                link = BATCHES + s.i
                dve.wait_ge(y_in[s.u], 16 * TOPK * (s.over(4) + (BATCHES // 4 + 1)))
                dve.tensor_tensor(xs, xs, Y[:, s.u, 0, :, :], ALU.add).then_inc(add_link, 1)
                dve.wait_ge(add_link, s.i + (BATCHES + 1))
                dve.tensor_tensor(xs, xs, Y[:, s.u, 1, :, :], ALU.add).then_inc(routed_added, 1)

            dve.wait_ge(sh_added, 2 * CHUNKS)
            pipelined(dve, [(add_last, 0)], BATCHES, 4)

        @block.scalar
        def _(act):
            act.wait_ge(consts, CONSTS)
            for l in range(2):
                def copy_xnT(s):
                    act.wait_ge(xnT_psum, s.i + (CHUNKS * l + 1))
                    act.activation(XNT[:, bass.ds(s.i * CH * P, CH * P)], psH[:, s.u, :], ACT.Copy)\
                       .then_inc(xnT_done, 1)

                def copy_logits(s):
                    act.wait_ge(logits_done, s.i + (CHUNKS * l + 1))
                    act.activation(logit[:, bass.ds(s.i * CH, CH), :],
                                   psY[:, :].rearrange("p (t e) -> p t e", t=CH)[:, :, 0:E], ACT.Copy)\
                       .then_inc(logits_out, 1)

                pipelined(act, [(copy_xnT, 0), (copy_logits, 1)], CHUNKS, 2)
                act.wait_ge(shifted, l + 1)
                act.activation(prob[:, :, :], cand[:, :, :], ACT.Exp).then_inc(expd, 1)

                def silu_of(s, base):
                    act.wait_ge(g_full, s.i + (base + 1))
                    if s.first + base >= 2:
                        act.wait_ge(h_done, s.i + (base - 1))
                    act.activation(silu[:, s.u % 2, :], psG[:, s.u % 2, :], ACT.Silu).then_inc(silu_done, 1)

                pipelined(act, [(lambda s: silu_of(s, first_shared[l]), 0)], SHARED, 2)

                def copy_hT(s):
                    act.wait_ge(hT_psum, s.i + (TILES_R * l + 1))
                    if s.past(2):
                        act.wait_ge(y_psum, s.i + (TILES_R * l - 1))
                    act.activation(hT[:, s.u % 2, :, :].rearrange("p j c -> p (j c)"), psH[:, s.u % 2, :],
                                   ACT.Copy).then_inc(hT_done, 1)

                pipelined(act, [(lambda s: silu_of(s, first_routed[l]), 0), (copy_hT, 1)], TILES_R, 2)

                if l == 1:
                    def store(s):
                        act.wait_ge(routed_added, s.i + (BATCHES + 1))
                        act.dma_start(out_v[:, bass.ds(s.i * TB, TB), :], X[:, bass.ds(s.i * TB, TB), :])\
                           .then_inc(out_sent, 16)

                    pipelined(act, [(store, 0)], BATCHES, 2)
                    act.wait_ge(out_sent, 16 * BATCHES)
                    continue

                def copy_anT(s):
                    act.wait_ge(anT_psum, s.i + 1)
                    if s.past(2):
                        act.wait_ge(qkv_psum, s.i - 1)
                    act.activation(anT[:, s.u, :], psT[:, 0:TB * P], ACT.Copy).then_inc(anT_done, 1)

                def squares(s):
                    act.wait_ge(qkv_psum, s.i + 1)
                    if s.past(2):
                        act.wait_ge(qk_scaled, s.i - 1)
                    for a in range(2):
                        for t in range(TB):
                            i = act.activation(sq[:, a, t, :], psQKV[s.u][:, t, a * D:(a + 1) * D], ACT.Square,
                                               scale=(2 - a) / D ** 0.5, accum_out=qk_ss[:, s.u, a, t:t + 1])
                    i.then_inc(ss_done, 1)

                def weights(s):
                    act.wait_ge(qk_scaled, s.i + 1)
                    if s.past(2):
                        act.wait_ge(ya_done, s.i - 1)
                    for t in range(TB):
                        act.activation(wkv[:, s.u, t, 0, :], psQKV[s.u][:, t, D:2 * D], ACT.Exp,
                                       scale=at_fac[:, s.u, 1, t:t + 1])
                    for t in range(TB):
                        i = act.activation(tq[:, s.u, t, :], psQKV[s.u][:, t, 0:D], ACT.Tanh,
                                           scale=at_fac[:, s.u, 0, t:t + 1])
                    i.then_inc(w_done, 1)

                def denominator(s):
                    act.wait_ge(cum_psum, s.i + 1)
                    if s.past(2):
                        act.wait_ge(ya_done, s.i - 1)
                    sums = psU[:, 0, :].rearrange("p (t a d) -> p t a d", t=TB, a=2)
                    act.activation(den[:, s.u, :, :], sums[:, :, 0, :], ACT.Copy, scale=2.0, bias=2e-6)\
                       .then_inc(den_done, 1)

                def copy_yT(s):
                    act.wait_ge(yT_psum, s.i + 1)
                    if s.past(2):
                        act.wait_ge(uv_psum, s.i - 1)
                    act.activation(yT[:, s.u, :], psT[:, TB * P:2 * TB * P], ACT.Copy).then_inc(yT_done, 1)

                def tanh_g(s):
                    act.wait_ge(uv_psum, s.i + 1)
                    act.activation(tg[:, s.u, :], psU[:, 1, 256:512], ACT.Tanh, scale=0.5).then_inc(tg_done, 1)

                stages = {"copy_yT": copy_yT, "tanh_g": tanh_g, "weights": weights, "copy_anT": copy_anT,
                          "squares": squares, "denominator": denominator}
                pipelined(act, [(stages[n], d) for n, d in ACT_STAGES], BATCHES, 2)

        @block.tensor
        def _(pe):
            pe.wait_ge(consts, CONSTS)
            pe.wait_ge(small_in, 64)

            def table_entry(j):
                return pe.value_load(w_off[0:1, bass.ds(j, 1)], min_val=0, max_val=(E - 1) * F)

            for l in range(2):
                for c in range(CHUNKS + 1):
                    if c < CHUNKS:
                        pe.wait_ge(xn_done, CHUNKS * l + c + 1)
                        if c >= 2:
                            pe.wait_ge(xnT_done, CHUNKS * l + c - 1)
                        for t in range(CH):
                            i = pe.transpose(psH[:, c % 2, t * P:(t + 1) * P], XN[:, c * CH + t, 0:D], ident[:, :])
                        i.then_inc(xnT_psum, 1)
                    if c > 0:
                        pe.wait_ge(xnT_done, CHUNKS * l + c)
                        if c > 1:
                            pe.wait_ge(logits_out, CHUNKS * l + c - 1)
                        for t in range(CH):
                            tok = ((c - 1) * CH + t) * P
                            i = pe.matmul(psY[:, t * P:(t + 1) * P], XNT[:, tok:tok + P], GATE[:, :],
                                          start=True, stop=True)
                        i.then_inc(logits_done, 1)

                def in_shared(s):
                    f = s.u % FT
                    chunk = XNT[:, bass.ds(s.over(FT) * CH * P, CH * P)]
                    if s.past(2):
                        pe.wait_ge(silu_done, s.i + (first_shared[l] - 1))
                    pe.matmul(psG[:, s.u % 2, :], W1S[:, f * P:(f + 1) * P], chunk, start=True, stop=True)\
                      .then_inc(g_full, 1)
                    if s.past(2):
                        pe.wait_ge(h_done, s.i + (first_shared[l] - 1))
                    pe.matmul(psU[:, s.u % 2, :], W3S[:, f * P:(f + 1) * P], chunk, start=True, stop=True)\
                      .then_inc(u_full, 1)

                def out_shared(s):
                    if s.u % FT:
                        return
                    c, par = s.over(FT), s.u // FT
                    pe.wait_ge(h_done, s.i + (first_shared[l] + FT))
                    if s.past(2 * FT):
                        pe.wait_ge(sh_added, c + (CHUNKS * l - 1))
                    for t in range(CH):
                        for f in range(FT):
                            i = pe.matmul(psH[:, par, t * D:(t + 1) * D], hs[:, par, f, t * P:(t + 1) * P],
                                          W2S[:, f, :], start=(f == 0), stop=(f == FT - 1))
                    i.then_inc(sh_full, 1)

                def rank():
                    pe.wait_ge(picked, l + 1)
                    flat = chosen16[:, :, :].rearrange("p i e -> p (i e)")
                    pe.matmul(psY[:, 0:TILES * E], before[:, :], flat, start=True, stop=True)
                    pe.matmul(psY[:, TILES * E:2 * TILES * E], ones16[:, :], flat, start=True, stop=True)\
                      .then_inc(ranked, 1)

                pipelined(pe, [(in_shared, 0), (out_shared, 5)], SHARED, 2 * FT, at={5: rank})
                pe.wait_ge(w_off_done, l + 1)
                pe.wait_ge(experts_in, 48)
                pe.wait_ge(ranks_read, l + 1)
                pe.wait_ge(sh_added, CHUNKS * (l + 1))

                def transpose_rows(s):
                    if s.u % GT:
                        return
                    g, par = s.over(GT), s.u // GT
                    pe.wait_ge(rows_in[par], 16 * (s.over(2 * GT) + (l * GROUPS // 2 + 1)))
                    if s.past(2):
                        pe.wait_ge(xT_done, g + GROUPS * l)
                    for t in range(GT):
                        i = pe.transpose(psT[:, t * P:(t + 1) * P], rows[:, par, t, 0:D], ident[:, :])
                    i.then_inc(xT_psum, 1)

                def in_routed(s):
                    par = s.u // GT
                    tile = xT[:, par, s.u % GT, :]
                    at = table_entry(s.i)
                    if s.u % GT == 0:
                        pe.wait_ge(xT_done, s.over(GT) + (GROUPS * l + 1))
                    pe.wait_ge(silu_done, s.i + (first_routed[l] - 1))
                    pe.matmul(psG[:, s.u % 2, :], tile, W1[:, bass.ds(at, F)], start=True, stop=True)\
                      .then_inc(g_full, 1)
                    pe.wait_ge(h_done, s.i + (first_routed[l] - 1))
                    pe.matmul(psU[:, s.u % 2, :], tile, W3[:, bass.ds(at, F)], start=True, stop=True)\
                      .then_inc(u_full, 1)

                def transpose_h(s):
                    pe.wait_ge(h_done, s.i + (first_routed[l] + 1))
                    if s.past(2):
                        pe.wait_ge(hT_done, s.i + (TILES_R * l - 1))
                    for f in range(FT):
                        i = pe.transpose(psH[:, s.u % 2, f * P:(f + 1) * P], hr[:, s.u % 2, f * P:(f + 1) * P],
                                         ident[:, :])
                    i.then_inc(hT_psum, 1)

                def out_routed(s):
                    at = table_entry(s.i)
                    pe.wait_ge(hT_done, s.i + (TILES_R * l + 1))
                    if s.u % GT == 0 and s.past(GT):
                        pe.wait_ge(y_done, s.over(GT) + GROUPS * l)
                    t = s.u % GT
                    for f in range(FT):
                        i = pe.matmul(psY[:, t * D:(t + 1) * D], hT[:, s.u % 2, f, :],
                                      W2[:, bass.ds(at + f * D, D)], start=(f == 0), stop=(f == FT - 1))
                    i.then_inc(y_psum, 1)

                pipelined(pe, [(in_routed, 2), (transpose_h, 3), (out_routed, 4), (transpose_rows, 0)],
                          TILES_R, 2 * GT)
                if l == 1:
                    continue
                pe.wait_ge(attn_in, 48)

                order = [n for n, _ in PE_STAGES]
                lag = dict(PE_STAGES)
                apart = lag["transpose_y"] - lag["transpose_xn"]
                y_first = order.index("transpose_y") < order.index("transpose_xn")

                def transpose_xn(s):
                    pe.wait_ge(xn_ready, s.i + 1)
                    issued = s.i + ((1 if y_first else 0) - apart)
                    if not isinstance(issued, int) or issued > 0:
                        pe.wait_ge(yT_done, issued)
                    if s.past(1):
                        pe.wait_ge(anT_done, s.i)
                    for t in range(TB):
                        i = pe.transpose(psT[:, t * P:(t + 1) * P], xn[:, s.u, t, :], ident[:, :])
                    i.then_inc(anT_psum, 1)

                def qkv(s):
                    pe.wait_ge(anT_done, s.i + 1)
                    if s.past(2):
                        pe.wait_ge(kv_done, s.i - 1)
                    for t in range(TB):
                        i = pe.matmul(psQKV[s.u][:, t, 0:3 * D], anT[:, s.u, t * P:(t + 1) * P], WQKV[:, :],
                                      start=True, stop=True)
                    i.then_inc(qkv_psum, 1)

                def cumulate(s):
                    pe.wait_ge(kv_done, s.i + 1)
                    if s.past(1):
                        pe.wait_ge(ya_done, s.i)
                    part = [wkv[:, s.u, t, :, :].rearrange("p a d -> p (a d)") for t in range(TB)]
                    pe.matmul(psU[:, 0, 0:256], upto[:, :], part[0], start=True, stop=True)
                    pe.matmul(psU[:, 0, 256:512], ones[:, :], part[0], start=True, stop=False)
                    pe.matmul(psU[:, 0, 256:512], upto[:, :], part[1], start=False, stop=True)\
                      .then_inc(cum_psum, 1)

                def transpose_y(s):
                    pe.wait_ge(ya_done, s.i + 1)
                    issued = s.i + ((0 if y_first else 1) + apart)
                    if isinstance(issued, int):
                        issued = min(issued, BATCHES)
                    pe.wait_ge(anT_done, issued)
                    if s.past(1):
                        pe.wait_ge(yT_done, s.i)
                    for t in range(TB):
                        i = pe.transpose(psT[:, (TB + t) * P:(TB + t + 1) * P], ya[:, s.u, t, :], ident[:, :])
                    i.then_inc(yT_psum, 1)

                def swiglu(s):
                    pe.wait_ge(yT_done, s.i + 1)
                    if s.past(1):
                        pe.wait_ge(ha_done, s.i)
                    for a in range(2):
                        i = pe.matmul(psU[:, 1, a * 256:(a + 1) * 256], WSW[:, a * D:(a + 1) * D], yT[:, s.u, :],
                                      start=True, stop=True)
                    i.then_inc(uv_psum, 1)

                def project(s):
                    pe.wait_ge(ha_done, s.i + 1)
                    if s.past(1):
                        pe.wait_ge(at_added, s.i)
                    for t in range(TB):
                        i = pe.matmul(psY[:, t * D:(t + 1) * D], ha[:, s.u, t * P:(t + 1) * P], WOUT[:, :],
                                      start=True, stop=True)
                    i.then_inc(at_psum, 1)

                stages = {"project": project, "transpose_y": transpose_y, "swiglu": swiglu, "cumulate": cumulate,
                          "transpose_xn": transpose_xn, "qkv": qkv}
                pipelined(pe, [(stages[n], d) for n, d in PE_STAGES], BATCHES, 2)


_INS = ["x", "w_qkvT", "w_swigluT", "w_outT", "gateT", "w1_e", "w3_e", "w2_e", "w1_s", "w3_s", "w2_s"]


def kernel(L0_attn_x, L0_attn_w_qkv, L0_attn_w_swiglu, L0_attn_w_out, L0_ffn_gate_W, L0_ffn_w1_e,
           L0_ffn_w3_e, L0_ffn_w2_e, L0_ffn_w1_s, L0_ffn_w3_s, L0_ffn_w2_s):
    import numpy as np
    import concourse.bacc as bacc
    from concourse.bass_utils import run_bass_kernel_spmd

    def lay(a):
        return np.ascontiguousarray(a)

    x = np.asarray(L0_attn_x)
    gateT = np.zeros((D, P), np.float32)
    gateT[:, :E] = np.asarray(L0_ffn_gate_W).T
    w1, w3, w2 = (np.asarray(a) for a in (L0_ffn_w1_e, L0_ffn_w3_e, L0_ffn_w2_e))
    arrays = {
        "x": lay(x.reshape(NT, D)),
        "w_qkvT": lay(np.asarray(L0_attn_w_qkv).T),
        "w_swigluT": lay(np.asarray(L0_attn_w_swiglu).T),
        "w_outT": lay(np.asarray(L0_attn_w_out).T),
        "gateT": gateT,
        "w1_e": lay(w1.transpose(1, 0, 2).reshape(D, E * F)),
        "w3_e": lay(w3.transpose(1, 0, 2).reshape(D, E * F)),
        "w2_e": lay(w2.reshape(E, FT, P, D).transpose(2, 0, 1, 3).reshape(P, E * FT * D)),
        "w1_s": lay(np.asarray(L0_ffn_w1_s).transpose(1, 0, 2).reshape(D, F)),
        "w3_s": lay(np.asarray(L0_ffn_w3_s).transpose(1, 0, 2).reshape(D, F)),
        "w2_s": lay(np.asarray(L0_ffn_w2_s).reshape(F, D)),
    }
    nc = bacc.Bacc("TRN2", target_bir_lowering=False, num_devices=1)
    args = [nc.dram_tensor(n, list(arrays[n].shape), fp32, kind="ExternalInput").ap() for n in _INS]
    out = nc.dram_tensor("out", [NT, D], fp32, kind="ExternalOutput").ap()
    macaron(nc, *args, out)
    result = run_bass_kernel_spmd(nc, [arrays], core_ids=[0]).results[0]
    return result["out"].reshape(x.shape)
```

```python
import concourse.bass as bass
from concourse import mybir
from contextlib import ExitStack

P = 128
D = 128
NT = 4096
TILES = NT // P
E = 8
TOPK = 2
F = 512
FT = F // P
CH = 4
CHUNKS = TILES // CH
SEQ = 256
BATCHES = NT // SEQ
TB = SEQ // P
TILES_R = TOPK * NT // P + E
GT = 4
GROUPS = TILES_R // GT
BATCH = 4
DEEP = 4
BATCHES_P = TOPK * TILES // BATCH
LN_EPS = 1e-5
RMS_EPS = 1.1920929e-07
NS = 8
WCOLS = 1024
WPARTS = E * F // WCOLS

EARLY = ({c: 1 for c in range(5, CHUNKS + 1)}, {})
EARLY_LAG = 2
LOW_LAG = (4, CHUNKS)
TAKEN = [sum(e.values()) for e in EARLY]
RANK_STEP = [n + 6 for n in TAKEN]
PLAN = [{n + 10 + step: 1 + step % 2 for step in range(11)} for n in TAKEN]
PLAN_LAG = 3
TABLE_STEP = [n + 23 for n in TAKEN]
EXPERTS_STEP = [n + 25 for n in TAKEN]

POOL_CHUNKS = (1, 4)

POOL_STAGES = [("qkv_rsqrt", 5), ("residual", 5), ("at_rsqrt", 3), ("mean_square", 4), ("add_routed", 1)]
DVE_STAGES = [("at_normalise", 4), ("at_aggregate", 3), ("gate_g", 8), ("at_statistics", 2), ("gate_u", 8),
              ("invert", 6), ("scale_q", 6), ("weigh_v", 5), ("attend", 6), ("add_attention", 9)]
ACT_STAGES = [("tanh_g", 8), ("gate_results", 0), ("denominator", 6), ("copy_yT", 7), ("copy_anT", 4),
              ("weights", 5), ("squares", 4)]
PE_STAGES = [("cumulate", 6), ("transpose_y", 7), ("project", 9), ("transpose_xn", 4), ("qkv", 4),
             ("swiglu", 7)]

LN_STEPS = {}
for c in range(CHUNKS - 1):
    added = CH // TB * (c + 1) + dict(DVE_STAGES)["add_attention"]
    LN_STEPS.setdefault(max(BATCHES + max(c - 1, 0), added), []).append(c)
POOL_END = BATCHES + max(lag for _, lag in POOL_STAGES)
POOL_AHEAD = sum(len(chunks) for k, chunks in LN_STEPS.items() if k < POOL_END)
LN_AHEAD = sum(len(chunks) for chunks in LN_STEPS.values())

fp32 = mybir.dt.float32
fp32r = mybir.dt.float32r
bf16 = mybir.dt.bfloat16
i32 = mybir.dt.int32
ALU = mybir.AluOpType
ACT = mybir.ActivationFunctionType
X_AXIS = mybir.AxisListType.X


class Step:

    def __init__(self, r, u, unroll, first):
        self.r, self.u, self.unroll, self.first = r, u, unroll, first
        self.i = r * unroll + u

    @classmethod
    def of(cls, i, unroll):
        return cls(i // unroll, i % unroll, unroll, i)

    def past(self, n):
        return self.first >= n or not isinstance(self.r, int)

    def over(self, n):
        return self.r * (self.unroll // n) + self.u // n


def pipelined(eng, stages, count, unroll, guard=2, at=None):
    deepest = max(d for _, d in stages)
    head = -(-(deepest + guard) // unroll) * unroll

    def static(k):
        if at and k in at:
            at[k]()
        for stage, d in stages:
            i = k - d
            if 0 <= i < count:
                stage(Step.of(i, unroll))

    for k in range(min(head, count)):
        static(k)
    if count > head:
        with eng.Fori(0, (count - head) // unroll) as r:
            for u in range(unroll):
                for stage, d in stages:
                    k = head + u - d
                    stage(Step(r + k // unroll, k % unroll, unroll, k))
    for k in range(count, count + deepest):
        static(k)


class Chain:

    def __init__(self, eng, sem):
        self.eng, self.sem, self.n = eng, sem, 0

    def then(self, instruction):
        instruction.then_inc(self.sem, 1)
        self.n += 1
        self.eng.wait_ge(self.sem, self.n)


def macaron(nc, x, w_qkvT, w_swigluT, w_outT, gateT, w1_e, w3_e, w2_e, w1_s, w3_s, w2_s, out):
    ctx = ExitStack()
    with ctx:
        def sb(name, shape, dt=fp32):
            return ctx.enter_context(nc.sbuf_tensor(name, shape, dt))

        def ps(name, shape, dt=fp32):
            return ctx.enter_context(nc.psum_tensor(name, shape, dt))

        def sem(name):
            return ctx.enter_context(nc.semaphore(name))

        tokens = nc.dram_tensor("tokens", [NT, D], fp32, kind="Internal").ap()
        results = nc.dram_tensor("results", [(TOPK * TILES + TILES_R) * P, D], fp32, kind="Internal").ap()

        def overlaid(*groups):
            handles = {}
            for group in groups[:-1]:
                with ExitStack() as lent:
                    for name, shape, dt in group:
                        handles[name] = lent.enter_context(nc.sbuf_tensor(name, shape, dt))
            for name, shape, dt in groups[-1]:
                handles[name] = sb(name, shape, dt)
            return handles

        X = sb("X", [P, TILES, D])
        W13H = sb("W13H", [P, 2, E * F], fp32r)
        memory = overlaid([("W13", [P, 2, E * F], fp32)], [("W13L", [P, 2, E * F], fp32r)])
        W13, W13L = memory["W13"], memory["W13L"]
        W2 = sb("W2", [P, E * FT * D])
        W13SH = sb("W13SH", [P, 2, F], fp32r)
        memory = overlaid([("W13S", [P, 2, F], fp32)], [("W13SL", [P, 2, F], fp32r)])
        W13S, W13SL = memory["W13S"], memory["W13SL"]
        W2S = sb("W2S", [P, FT, D])
        GATE = sb("GATE", [P, P])
        WQKV = sb("WQKV", [P, 3 * D])
        WSW = sb("WSW", [P, 2 * D])
        WOUT = sb("WOUT", [P, D])
        ident = sb("ident", [P, P])
        ones = sb("ones", [P, P])
        upto = sb("upto", [P, P])
        before = sb("before", [P, P], bf16)
        ones16 = sb("ones16", [P, P], bf16)
        rev_e = sb("rev_e", [P, E])
        tile_starts = sb("tile_starts", [P, TILES])
        tile_no = sb("tile_no", [P, TILES_R])
        own_row = sb("own_row", [P, TILES_R])
        column = sb("column", [P, P], bf16)
        partition = sb("partition", [P, 1])
        minus_half = sb("minus_half", [P, 3 * TB])
        rms_eps = sb("rms_eps", [P, 2, TB])
        ln_stats = sb("ln_stats", [P, 2, CH, 6])
        ln_mv = sb("ln_mv", [P, 2, CH, 2])
        ln_var = sb("ln_var", [P, 2, CH])
        ln_rstd = sb("ln_rstd", [P, 2, CH])
        chosen16 = sb("chosen16", [P, TILES, E], bf16)
        row_a = sb("row_a", [P, TILES])
        row_b = sb("row_b", [P, TILES])
        top = [sb(f"top{k}", [P, TILES]) for k in range(TOPK)]
        cnt = sb("cnt", [P, E])
        ntile = sb("ntile", [P, E])
        tend = sb("tend", [P, E])
        tstart = sb("tstart", [P, E])
        shift = sb("shift", [P, E])
        tile_e = sb("tile_e", [P, TILES_R])
        w_off = sb("w_off", [P, TILES_R], i32)
        posf = sb("posf", [P, TILES])
        pos = sb("pos", [P, TOPK, TILES], i32)
        pos_bits = sb("pos_bits", [P, 2, TOPK, TILES], i32)
        pos_part = sb("pos_part", [P, 2, TOPK * TILES])
        gates = sb("gates", [P, TOPK, TILES])
        found = sb("found", [P, TILES_R])
        spare = sb("spare", [P, TILES_R])
        source = sb("source", [P, TILES_R], i32)
        target = sb("target", [P, TILES_R], i32)
        source_now = sb("source_now", [P, 2, GT], i32)
        target_now = sb("target_now", [P, 2, GT], i32)
        at_stats = sb("at_stats", [P, 2, TB, 6])
        at_mv = sb("at_mv", [P, 2, TB, 2])
        at_var = sb("at_var", [P, 2, 2, TB])
        at_rstd = sb("at_rstd", [P, 2, TB])
        at_sq = sb("at_sq", [P, 2, TB])
        at_eps = sb("at_eps", [P, 2, 2, TB])
        at_ms = sb("at_ms", [P, 2, 3, TB])
        at_fac = sb("at_fac", [P, 2, 3, TB])
        qk_ss = sb("qk_ss", [P, 2, 2, TB])
        memory = overlaid(
            [("xTH", [P, 2, GT, P], fp32r), ("xTL", [P, 2, GT, P], fp32r)],
            [(name, [P, TILES, E], fp32) for name in ("logit", "prob", "cand", "onehot0", "onehot1")] +
            [(name, [P, E, TILES], fp32) for name in ("tot", "cum", "excl", "pick", "need")] +
            [("tile_cmp", [P, TILES_R, E], fp32)])
        xTH = memory["xTH"]
        xTL = memory["xTL"]
        logit = memory["logit"]
        prob = memory["prob"]
        cand = memory["cand"]
        onehot = [memory[f"onehot{k}"] for k in range(TOPK)]
        tot = memory["tot"]
        cum = memory["cum"]
        excl = memory["excl"]
        pick = memory["pick"]
        need = memory["need"]
        tile_cmp = memory["tile_cmp"]
        memory = overlaid(
            [("rows", [P, 2, GT, D], fp32),
             ("hr", [P, 2, F], fp32),
             ("hT", [P, 2, FT, P], fp32),
             ("yout", [P, 2, GT, D], fp32)],
            [("XN", [P, TILES, D], fp32)])
        rows = memory["rows"]
        hr = memory["hr"]
        hT = memory["hT"]
        yout = memory["yout"]
        XN = memory["XN"]
        memory = overlaid(
            [("Y", [P, 4, TOPK, TB, D], fp32)],
            [("hs", [P, 2, FT, CH * P], fp32),
             ("silu", [P, 2, F], fp32),
             ("at_place", [P, DEEP, BATCH, P], bf16),
             ("in_tile", [P, 2, BATCH, TILES_R], bf16),
             ("pair", [P, DEEP, BATCH, 2, TILES_R], bf16)])
        Y = memory["Y"]
        hs = memory["hs"]
        silu = memory["silu"]
        at_place = memory["at_place"]
        in_tile = memory["in_tile"]
        pair = memory["pair"]
        memory = overlaid(
            [("xn", [P, 2, TB, D], fp32),
             ("anT", [P, 2, TB * P], fp32),
             ("sq", [P, 2, TB, D], bf16),
             ("wkv", [P, 2, TB, 2, D], fp32),
             ("tq", [P, 2, TB, D], fp32),
             ("den", [P, 2, TB, D], fp32),
             ("rec", [P, 2, TB, D], fp32),
             ("ysc", [P, 2, TB, D], fp32),
             ("ya", [P, 2, TB, D], fp32),
             ("yT", [P, 2, TB * P], fp32),
             ("tg", [P, 2, TB * P], fp32),
             ("ag", [P, 2, TB * P], fp32),
             ("ha", [P, 2, TB * P], fp32)],
            [("YF", [P, TOPK, TILES, D], fp32)],
            [("XNT", [P, NT], fp32)],
            [("XNTL", [P, NT], fp32r), ("XNTH", [P, NT], fp32r)])
        xn = memory["xn"]
        anT = memory["anT"]
        sq = memory["sq"]
        wkv = memory["wkv"]
        tq = memory["tq"]
        den = memory["den"]
        rec = memory["rec"]
        ysc = memory["ysc"]
        ya = memory["ya"]
        yT = memory["yT"]
        tg = memory["tg"]
        ag = memory["ag"]
        ha = memory["ha"]
        XNTH = memory["XNTH"]
        XNTL = memory["XNTL"]
        XNT = memory["XNT"]
        YF = memory["YF"]

        psG = ps("psG", [P, 2, 512])
        psU = ps("psU", [P, 2, 512])
        psH = ps("psH", [P, 2, 512])
        psT = ps("psT", [P, 512])
        psY = ps("psY", [P, 512])

        x_in = [sem(f"x_in{c}") for c in range(CHUNKS)]
        small_in = sem("small_in")
        experts_in = sem("experts_in")
        attn_in = sem("attn_in")
        ws_high = sem("ws_high")
        ws_split = sem("ws_split")
        w_high = sem("w_high")
        w_split = sem("w_split")
        consts = sem("consts")
        const_link = sem("const_link")
        ln_link = sem("ln_link")
        ln_stat = sem("ln_stat")
        ln_scaled = sem("ln_scaled")
        xn_done = sem("xn_done")
        xnT_psum = sem("xnT_psum")
        xnT_done = sem("xnT_done")
        xnT_high = sem("xnT_high")
        xnT_split = sem("xnT_split")
        logits_done = sem("logits_done")
        logits_out = sem("logits_out")
        route_link = sem("route_link")
        shifted = sem("shifted")
        expd = sem("expd")
        picked = sem("picked")
        ranked = sem("ranked")
        ranks_read = sem("ranks_read")
        w_off_done = sem("w_off_done")
        tokens_out = sem("tokens_out")
        tile_made = sem("tile_made")
        place_made = sem("place_made")
        pair_made = sem("pair_made")
        batch_used = sem("batch_used")
        table_done = sem("table_done")
        g_full = sem("g_full")
        u_full = sem("u_full")
        silu_done = sem("silu_done")
        h_done = sem("h_done")
        sh_full = sem("sh_full")
        sh_added = sem("sh_added")
        rows_in = [sem(f"rows_in{p}") for p in range(2)]
        xT_psum = sem("xT_psum")
        xT_done = sem("xT_done")
        xT_link = sem("xT_link")
        table_link = sem("table_link")
        source_link = sem("source_link")
        target_link = sem("target_link")
        hT_psum = sem("hT_psum")
        hT_done = sem("hT_done")
        y_psum = sem("y_psum")
        y_done = sem("y_done")
        y_part = sem("y_part")
        y_sent = [sem(f"y_sent{p}") for p in range(2)]
        y_in = [sem(f"y_in{p}") for p in range(4)]
        yf_in = [sem(f"yf_in{c}") for c in range(CHUNKS)]
        y_scaled = sem("y_scaled")
        add_link = sem("add_link")
        last_link = sem("last_link")
        last_link_pool = sem("last_link_pool")
        last_added = sem("last_added")
        last_added_pool = sem("last_added_pool")
        routed_added = sem("routed_added")
        out_sent = sem("out_sent")
        at_link = sem("at_link")
        at_stat = sem("at_stat")
        sq_link = sem("sq_link")
        rms_terms = sem("rms_terms")
        at_scaled = sem("at_scaled")
        xn_ready = sem("xn_ready")
        xres_done = sem("xres_done")
        anT_psum = sem("anT_psum")
        anT_done = sem("anT_done")
        qkv_psum = sem("qkv_psum")
        ss_done = sem("ss_done")
        qk_scaled = sem("qk_scaled")
        w_done = sem("w_done")
        qk_link = sem("qk_link")
        kv_done = sem("kv_done")
        cum_psum = sem("cum_psum")
        den_done = sem("den_done")
        y_link = sem("y_link")
        ya_done = sem("ya_done")
        yT_psum = sem("yT_psum")
        yT_done = sem("yT_done")
        uv_psum = sem("uv_psum")
        tg_done = sem("tg_done")
        h_link = sem("h_link")
        ha_done = sem("ha_done")
        at_psum = sem("at_psum")
        at_added = sem("at_added")

        psQKV = [psG, psH]
        last_y = [psY, psT]

        block = ctx.enter_context(nc.Block())
        CONSTS = 13
        SHARED = CHUNKS * FT
        first_shared = [l * (SHARED + TILES_R) for l in range(2)]
        first_routed = [f + SHARED for f in first_shared]

        def wait_apart(eng, semaphore, value):
            if isinstance(value, int):
                eng.wait_ge(semaphore, value)
                return
            with eng.register() as wanted:
                eng.reg_mov(wanted, value)
                eng.wait_ge(consts, CONSTS)
                eng.wait_ge(semaphore, wanted)

        x_v = x.rearrange("(i p) d -> p i d", p=P)
        out_v = out.rearrange("(i p) d -> p i d", p=P)
        tokens_v = tokens.rearrange("(i p) d -> p i d", p=P)
        results_v = results[0:TOPK * NT, :].rearrange("(k i p) d -> p k i d", k=TOPK, p=P)

        @block.sync
        def _(sp):
            for c in range(CHUNKS):
                sp.dma_start(X[:, c * CH:(c + 1) * CH, :], x_v[:, c * CH:(c + 1) * CH, :]).then_inc(x_in[c], 16)
                if c == 1:
                    for dst, src in ((GATE[:, :], gateT), (W13S[:, 0, :], w1_s), (W13S[:, 1, :], w3_s),
                                     (W2S[:, :, :], w2_s.rearrange("(j p) d -> p j d", p=P))):
                        sp.dma_start(dst, src).then_inc(small_in, 16)
            for dst, src in ((W13[:, 0, :], w1_e), (W13[:, 1, :], w3_e), (W2[:, :], w2_e)):
                sp.dma_start(dst, src).then_inc(experts_in, 16)
            for dst, src in ((WQKV[:, :], w_qkvT), (WSW[:, :], w_swigluT), (WOUT[:, :], w_outT)):
                sp.dma_start(dst, src).then_inc(attn_in, 16)
            for l in range(2):
                def keep_tokens(s):
                    sp.wait_ge(xn_done, s.i + (l * CHUNKS + 1))
                    chunk = bass.ds(s.i * CH, CH)
                    sp.dma_start(tokens_v[:, chunk, :], XN[:, chunk, :]).then_inc(tokens_out, 16)

                pipelined(sp, [(keep_tokens, 0)], CHUNKS, 2)
                for p in range(2):
                    sp.wait_ge(y_sent[p], 16 * TILES_R // 2 * (l + 1))

                if l == 1:
                    for c in range(CHUNKS):
                        chunk = slice(c * CH, (c + 1) * CH)
                        for k in range(TOPK):
                            sp.dma_start(YF[:, k, chunk, :], results_v[:, k, chunk, :]).then_inc(yf_in[c], 16)
                    continue

                def load_results(s):
                    if s.past(4):
                        sp.wait_ge(routed_added, s.i - 3)
                    for k in range(TOPK):
                        sp.dma_start(Y[:, s.u, k, :, :], results_v[:, k, bass.ds(s.i * TB, TB), :])\
                          .then_inc(y_in[s.u], 16)

                pipelined(sp, [(load_results, 0)], BATCHES, 4)

        @block.gpsimd
        def _(pool):
            one = Chain(pool, const_link)
            pool.memset(ones[:, :], 1.0).then_inc(consts, 1)
            pool.memset(ones16[:, :], 1.0).then_inc(consts, 1)
            pool.memset(minus_half[:, :], -0.5).then_inc(consts, 1)
            pool.memset(rms_eps[:, 0, :], 4 * RMS_EPS).then_inc(consts, 1)
            pool.memset(rms_eps[:, 1, :], RMS_EPS).then_inc(consts, 1)
            one.then(pool.memset(ident[:, :], 0.0))
            one.then(pool.memset(upto[:, :], 1.0))
            one.then(pool.memset(before[:, :], 1.0))
            pool.affine_select(out=ident[:, :], in_=ident[:, :], compare_op=ALU.not_equal, fill=1.0,
                               base=0, pattern=[[-1, P]], channel_multiplier=1).then_inc(consts, 1)
            pool.affine_select(out=upto[:, :], in_=upto[:, :], compare_op=ALU.is_ge, fill=0.0,
                               base=0, pattern=[[1, P]], channel_multiplier=-1).then_inc(consts, 1)
            pool.affine_select(out=before[:, :], in_=before[:, :], compare_op=ALU.is_gt, fill=0.0,
                               base=0, pattern=[[1, P]], channel_multiplier=-1).then_inc(consts, 1)
            pool.iota(own_row[:, :], pattern=[[P, TILES_R]], base=TOPK * NT + P, channel_multiplier=1,
                      allow_small_or_imprecise_dtypes=True).then_inc(consts, 1)
            pool.iota(column[:, :], pattern=[[1, P]], base=0, channel_multiplier=0,
                      allow_small_or_imprecise_dtypes=True).then_inc(consts, 1)
            pool.iota(partition[:, :], pattern=[[0, 1]], base=0, channel_multiplier=1,
                      allow_small_or_imprecise_dtypes=True).then_inc(consts, 1)
            pool.iota(rev_e[:, :], pattern=[[-1, E]], base=E, channel_multiplier=0,
                      allow_small_or_imprecise_dtypes=True).then_inc(consts, 1)
            pool.iota(tile_starts[:, :], pattern=[[P, TILES]], base=0, channel_multiplier=0,
                      allow_small_or_imprecise_dtypes=True).then_inc(consts, 1)
            pool.iota(tile_no[:, :], pattern=[[1, TILES_R]], base=0, channel_multiplier=0,
                      allow_small_or_imprecise_dtypes=True).then_inc(consts, 1)
            pool.wait_ge(consts, CONSTS)

            def scale_ln(l, s):
                pool.wait_ge(ln_stat, s.i + (l * CHUNKS + 1))
                pool.tensor_tensor(ln_rstd[:, s.u, :], ln_var[:, s.u, :], minus_half[:, 0:CH], ALU.pow)\
                    .then_inc(ln_scaled, 1)

            def add_routed(s):
                xs = X[:, bass.ds(s.i * TB, TB), :]
                wait_apart(pool, y_scaled, s.i + 1)
                if s.first == 0:
                    pool.wait_ge(sh_added, CHUNKS)
                pool.tensor_tensor(xs, xs, Y[:, s.u % 4, 0, :, :], ALU.add).then_inc(add_link, 1)
                wait_apart(pool, add_link, s.i + 1)
                pool.tensor_tensor(xs, xs, Y[:, s.u % 4, 1, :, :], ALU.add).then_inc(routed_added, 1)

            for l in range(2):
                def low_xnT(s):
                    wait_apart(pool, xnT_high, s.i + (l * CHUNKS + 1))
                    chunk = bass.ds(s.i * CH * P, CH * P)
                    pool.tensor_tensor(XNTL[:, chunk], XNT[:, chunk], XNTH[:, chunk].bitcast(fp32), ALU.subtract)\
                        .then_inc(xnT_split, 1)

                def low_shared():
                    pool.wait_ge(ws_high, 1)
                    pool.tensor_tensor(W13SL[:, :, :], W13S[:, :, :], W13SH[:, :, :].bitcast(fp32), ALU.subtract)\
                        .then_inc(ws_split, 1)

                for c in range(CHUNKS + LOW_LAG[l]):
                    if c < CHUNKS and (l == 0 or c >= POOL_AHEAD):
                        scale_ln(l, Step.of(c, 2))
                    if l == 0 and c == 3:
                        low_shared()
                    if c >= LOW_LAG[l]:
                        low_xnT(Step.of(c - LOW_LAG[l], 2))

                if l == 0:
                    pool.wait_ge(experts_in, 48)
                    for j in range(2 * WPARTS):
                        w, cols = j % 2, bass.ds(j // 2 * WCOLS, WCOLS)
                        pool.tensor_copy(W13H[:, w, cols], W13[:, w, cols]).then_inc(w_high, 1)
                        pool.wait_ge(w_high, j + 1)
                        pool.tensor_tensor(W13L[:, w, cols], W13[:, w, cols],
                                           W13H[:, w, cols].bitcast(fp32), ALU.subtract).then_inc(w_split, 1)
                pool.wait_ge(tokens_out, 16 * CHUNKS * (l + 1))
                pool.wait_ge(table_done, l + 1)

                def fetch_rows(s):
                    if s.past(2):
                        wait_apart(pool, xT_psum, s.i + (l * GROUPS - 1))
                    pool.tensor_copy(source_now[:, s.u, :], source[:, bass.ds(s.i * GT, GT)])\
                        .then_inc(source_link, 1)
                    wait_apart(pool, source_link, s.i + (l * GROUPS + 1))
                    for t in range(GT):
                        pool.indirect_dma_start(
                            rows[:, s.u, t, :], None, tokens,
                            bass.IndirectOffsetOnAxis(ap=source_now[:, s.u, t:t + 1], axis=0))\
                            .then_inc(rows_in[s.u], 16)

                def send_results(s):
                    last = isinstance(s.i, int) and s.i == GROUPS - 1
                    if not last:
                        wait_apart(pool, y_done, s.i + (l * GROUPS + 1))
                    else:
                        pool.wait_ge(y_sent[s.u], 16 * GT * (GROUPS // 2 * (l + 1) - 1))
                    pool.tensor_copy(target_now[:, s.u, :], target[:, bass.ds(s.i * GT, GT)])\
                        .then_inc(target_link, 1)
                    wait_apart(pool, target_link, s.i + (l * GROUPS + 1))
                    for t in range(GT):
                        if last and t < GT - 1:
                            pool.wait_ge(y_part, (GT - 1) * l + t + 1)
                        elif last:
                            pool.wait_ge(y_done, GROUPS * (l + 1))
                        pool.indirect_dma_start(
                            results, bass.IndirectOffsetOnAxis(ap=target_now[:, s.u, t:t + 1], axis=0),
                            yout[:, s.u, t, :], None).then_inc(y_sent[s.u], 16)

                pipelined(pool, [(fetch_rows, 0), (send_results, 3)], GROUPS, 2, guard=1)

                def at_rsqrt(s):
                    pool.wait_ge(at_stat, s.i + 1)
                    pool.tensor_tensor(at_rstd[:, s.u % 2, :], at_var[:, s.u % 2, 0, :], minus_half[:, 0:TB], ALU.pow)\
                        .then_inc(at_scaled, 1)

                def mean_square(s):
                    pool.wait_ge(at_scaled, s.i + 1)
                    if s.past(2):
                        pool.wait_ge(qk_scaled, s.i - 1)
                    u = s.u % 2
                    pool.tensor_tensor(at_sq[:, u, :], at_rstd[:, u, :], at_rstd[:, u, :], ALU.mult)\
                        .then_inc(sq_link, 1)
                    pool.wait_ge(sq_link, s.i * 2 + 1)
                    pool.tensor_tensor(at_ms[:, u, 2, :], at_sq[:, u, :], at_var[:, u, 1, :], ALU.mult)\
                        .then_inc(sq_link, 1)
                    pool.wait_ge(sq_link, s.i * 2 + 2)
                    pool.tensor_tensor(at_eps[:, u, :, :], at_ms[:, u, 2, :].unsqueeze(1).to_broadcast([P, 2, TB]),
                                       rms_eps[:, :, :], ALU.mult).then_inc(rms_terms, 1)

                def residual(s):
                    wait_apart(pool, xn_ready, s.i + 1)
                    xs = X[:, bass.ds(s.i * TB, TB), :]
                    pool.tensor_tensor(xs, xs, xn[:, s.u % 2, :, :], ALU.add).then_inc(xres_done, 1)

                def qkv_rsqrt(s):
                    pool.wait_ge(ss_done, s.i + 1)
                    pool.wait_ge(rms_terms, s.i + 1)
                    if s.past(2):
                        pool.wait_ge(kv_done, s.i - 1)
                    ms = at_ms[:, s.u % 2, :, :]
                    pool.tensor_tensor(ms[:, 0:2, :], qk_ss[:, s.u % 2, :, :], at_eps[:, s.u % 2, :, :], ALU.add)\
                        .then_inc(qk_link, 1)
                    pool.wait_ge(qk_link, s.i + 1)
                    pool.tensor_tensor(at_fac[:, s.u % 2, :, :], ms, minus_half[:, 0:3 * TB]
                                       .rearrange("p (a t) -> p a t", a=3), ALU.pow).then_inc(qk_scaled, 1)

                if l == 0:
                    stages = {"qkv_rsqrt": qkv_rsqrt, "add_routed": add_routed, "residual": residual,
                              "at_rsqrt": at_rsqrt, "mean_square": mean_square}

                    def scale_ahead(chunks):
                        def run():
                            for c in chunks:
                                scale_ln(1, Step.of(c, 2))
                        return run

                    pipelined(pool, [(stages[n], d) for n, d in POOL_STAGES], BATCHES, 4,
                              at={k: scale_ahead(chunks) for k, chunks in LN_STEPS.items() if k < POOL_END})

            link = Chain(pool, last_link_pool)
            for c in POOL_CHUNKS:
                pool.wait_ge(yf_in[c], 16 * TOPK)
                chunk = slice(c * CH, (c + 1) * CH)
                ys, xs = YF[:, :, chunk, :], X[:, chunk, :]
                link.then(pool.tensor_tensor(ys, ys, gates[:, :, chunk].unsqueeze(3).to_broadcast([P, TOPK, CH, D]),
                                             ALU.mult))
                link.then(pool.tensor_tensor(xs, xs, ys[:, 0, :, :], ALU.add))
                pool.tensor_tensor(xs, xs, ys[:, 1, :, :], ALU.add).then_inc(last_added_pool, 1)

        @block.vector
        def _(dve):
            dve.wait_ge(consts, CONSTS)
            route = Chain(dve, route_link)

            def wide(ap, shape):
                return ap.unsqueeze(2).to_broadcast(shape)

            TE = [P, TILES, E]
            ET = [P, E, TILES]
            def stats(l, s):
                if l == 0:
                    dve.wait_ge(x_in[s.i], 16)
                else:
                    dve.wait_ge(at_added, CH // TB * (s.i + 1))
                base = 2 * CHUNKS * l
                for t in range(CH):
                    i = dve.bn_stats(ln_stats[:, s.u % 2, t, :], X[:, s.i * CH + t, :])
                i.then_inc(ln_link, 1)
                dve.wait_ge(ln_link, base + 2 * s.i + 1)
                for t in range(CH):
                    i = dve.bn_aggr(ln_mv[:, s.u % 2, t, :], ln_stats[:, s.u % 2, t, :])
                i.then_inc(ln_link, 1)
                dve.wait_ge(ln_link, base + 2 * s.i + 2)
                dve.tensor_scalar(ln_var[:, s.u % 2, :], ln_mv[:, s.u % 2, :, 1], LN_EPS, None, ALU.add)\
                   .then_inc(ln_stat, 1)

            def normalise(l, s):
                dve.wait_ge(ln_scaled, s.i + (l * CHUNKS + 1))
                for t in range(CH):
                    i = dve.tensor_scalar(XN[:, s.i * CH + t, :], X[:, s.i * CH + t, :],
                                          ln_mv[:, s.u % 2, t, 0:1], ln_rstd[:, s.u % 2, t:t + 1],
                                          ALU.subtract, ALU.mult)
                i.then_inc(xn_done, 1)

            for l in range(2):
                def gated(hidden, s, base):
                    dve.wait_ge(silu_done, s.i + (base + 1))
                    dve.wait_ge(u_full, s.i + (base + 1))
                    dve.tensor_tensor(hidden, silu[:, s.u % 2, :], psU[:, s.u % 2, :], ALU.mult).then_inc(h_done, 1)

                def gated_shared(s):
                    if s.past(2 * FT) and s.u % FT == 0:
                        dve.wait_ge(sh_full, s.over(FT) + (CHUNKS * l - 1))
                    gated(hs[:, s.u // FT, s.u % FT, :], s, first_shared[l])

                def add_shared(c):
                    dve.wait_ge(sh_full, c + (CHUNKS * l + 1))
                    xs = X[:, c * CH:(c + 1) * CH, :].rearrange("p t d -> p (t d)")
                    dve.scalar_tensor_tensor(xs, psH[:, c % 2, :], 0.25 / NS, xs, ALU.mult, ALU.add)\
                       .then_inc(sh_added, 1)

                done = [0]

                def shared_steps(n):
                    for _ in range(n):
                        k = done[0]
                        gated_shared(Step.of(k, 2 * FT))
                        done[0] += 1
                        if k >= 6 and k % FT == 6 % FT:
                            add_shared(k // FT - 1)

                for c in range(CHUNKS + 1 + EARLY_LAG):
                    if c < CHUNKS and (l == 0 or c >= LN_AHEAD):
                        stats(l, Step.of(c, 2))
                    if 0 < c <= CHUNKS and (l == 0 or c >= LN_AHEAD):
                        normalise(l, Step.of(c - 1, 2))
                    if l == 0:
                        shared_steps(EARLY[l].get(c - EARLY_LAG, 0))
                if l == 1:
                    shared_steps(TAKEN[1])

                dve.wait_ge(logits_out, CHUNKS * (l + 1))
                route.then(dve.tensor_reduce(row_a[:, :], logit[:, :, :], X_AXIS, ALU.max))
                dve.tensor_tensor(cand[:, :, :], logit[:, :, :], wide(row_a[:, :], TE), ALU.subtract)\
                   .then_inc(shifted, 1)
                shared_steps(1)
                dve.wait_ge(expd, l + 1)
                route.then(dve.tensor_reduce(row_b[:, :], prob[:, :, :], X_AXIS, ALU.add))
                route.then(dve.reciprocal(row_a[:, :], row_b[:, :]))
                route.then(dve.tensor_tensor(prob[:, :, :], prob[:, :, :], wide(row_a[:, :], TE), ALU.mult))
                shared_steps(1)
                for k in range(TOPK):
                    if k == 1:
                        shared_steps(1)
                    route.then(dve.tensor_reduce(top[k][:, :], prob[:, :, :], X_AXIS, ALU.max))
                    route.then(dve.tensor_tensor(cand[:, :, :], prob[:, :, :], wide(top[k][:, :], TE), ALU.is_ge))
                    route.then(dve.tensor_tensor(cand[:, :, :], cand[:, :, :],
                                                 rev_e[:, :].unsqueeze(1).to_broadcast(TE), ALU.mult))
                    if k == 1:
                        shared_steps(1)
                    route.then(dve.tensor_reduce(row_b[:, :], cand[:, :, :], X_AXIS, ALU.max))
                    route.then(dve.tensor_tensor(onehot[k][:, :, :], rev_e[:, :].unsqueeze(1).to_broadcast(TE),
                                                 wide(row_b[:, :], TE), ALU.is_equal))
                    if k == 0:
                        shared_steps(1)
                        route.then(dve.scalar_tensor_tensor(prob[:, :, :], onehot[0][:, :, :], -2.0,
                                                            prob[:, :, :], ALU.mult, ALU.add))
                dve.tensor_tensor(chosen16[:, :, :], onehot[0][:, :, :], onehot[1][:, :, :], ALU.add)\
                   .then_inc(picked, 1)
                shared_steps(2)

                def slots_of():
                    dve.wait_ge(ranked, l + 1)
                    within = psY[:, 0:TILES * E].rearrange("p (i e) -> p e i", e=E)
                    totals = psY[:, TILES * E:2 * TILES * E].rearrange("p (i e) -> p e i", e=E)
                    route.then(dve.tensor_copy(tot[:, :, :], totals))
                    flat = "p e i -> p (e i)"
                    route.then(dve.tensor_tensor_scan(cum[:, :, :].rearrange(flat), ones[:, 0:1].to_broadcast([P, E * TILES]),
                                                      tot[:, :, :].rearrange(flat), 0.0, ALU.mult, ALU.add))
                    route.then(dve.tensor_tensor(excl[:, :, :], cum[:, :, :], tot[:, :, :], ALU.subtract))
                    route.then(dve.tensor_tensor(cnt[:, :], cum[:, :, TILES - 1], excl[:, :, 0], ALU.subtract))
                    shared_steps(1)
                    route.then(dve.tensor_tensor(need[:, :, :], wide(cnt[:, :], ET),
                                                 tile_starts[:, :].unsqueeze(1).to_broadcast(ET), ALU.is_gt))
                    route.then(dve.tensor_reduce(ntile[:, :], need[:, :, :], X_AXIS, ALU.add))
                    route.then(dve.tensor_tensor_scan(tend[:, :], ones[:, 0:E], ntile[:, :], 0.0,
                                                      ALU.mult, ALU.add))
                    route.then(dve.tensor_tensor(tstart[:, :], tend[:, :], ntile[:, :], ALU.subtract))
                    shared_steps(1)
                    route.then(dve.scalar_tensor_tensor(shift[:, :], tstart[:, :], float(P), excl[:, :, 0],
                                                        ALU.mult, ALU.subtract))
                    route.then(dve.tensor_tensor(excl[:, :, :], excl[:, :, :], wide(shift[:, :], ET), ALU.add))
                    i = dve.tensor_tensor(excl[:, :, :], excl[:, :, :], within, ALU.add)
                    i.then_inc(ranks_read, 1)
                    dve.wait_ge(ranks_read, l + 1)
                    for k in range(TOPK):
                        route.then(dve.tensor_tensor(pick[:, :, :], excl[:, :, :],
                                                     onehot[k][:, :, :].rearrange("p i e -> p e i"), ALU.mult))
                        route.then(dve.tensor_reduce(posf[:, :], pick[:, :, :].rearrange("p e i -> p i e"),
                                                     X_AXIS, ALU.add))
                        route.then(dve.tensor_copy(pos[:, k, :], posf[:, :]))
                        shared_steps(1)
                    dve.tensor_scalar(pos_bits[:, 0, :, :], pos[:, :, :], P - 1, None, ALU.bitwise_and)
                    route.then(dve.tensor_scalar(pos_bits[:, 1, :, :], pos[:, :, :], P.bit_length() - 1, None,
                                                 ALU.logical_shift_right))
                    route.then(dve.tensor_copy(pos_part[:, :, :],
                                               pos_bits[:, :, :, :].rearrange("p a k i -> p a (k i)")))

                def batch(b):
                    at = slice(b * BATCH, (b + 1) * BATCH)
                    if b >= 2:
                        dve.wait_ge(pair_made, BATCHES_P * l + b - 1)
                    if b >= DEEP:
                        dve.wait_ge(batch_used, BATCHES_P * l + b - DEEP + 1)
                    cmp3 = [P, BATCH, TILES_R]
                    dve.tensor_tensor(in_tile[:, b % 2, :, :], column[:, 0:TILES_R].unsqueeze(1).to_broadcast(cmp3),
                                      wide(pos_part[:, 1, at], cmp3), ALU.is_equal).then_inc(tile_made, 1)
                    for m in range(BATCH):
                        i = dve.tensor_scalar(at_place[:, b % DEEP, m, :], column[:, :],
                                              pos_part[:, 0, b * BATCH + m:b * BATCH + m + 1], None, ALU.is_equal)
                    i.then_inc(place_made, 1)

                def experts():
                    for k in range(TOPK):
                        dve.tensor_scalar(gates[:, k, :], top[k][:, :], 0.25, None, ALU.mult)
                    cmp3 = [P, TILES_R, E]
                    route.then(dve.tensor_tensor(tile_cmp[:, :, :], wide(tile_no[:, :], cmp3),
                                                 tend[:, :].unsqueeze(1).to_broadcast(cmp3), ALU.is_ge))
                    route.then(dve.tensor_reduce(tile_e[:, :], tile_cmp[:, :, :], X_AXIS, ALU.add))
                    dve.tensor_scalar(w_off[:, :], tile_e[:, :], float(E - 1), float(F),
                                      ALU.min, ALU.mult).then_inc(w_off_done, 1)

                def table():
                    dve.wait_ge(batch_used, BATCHES_P * (l + 1))
                    place, rest = psT[:, 0:TILES_R], psT[:, TILES_R:2 * TILES_R]
                    route.then(dve.tensor_copy(spare[:, :], place))
                    route.then(dve.scalar_tensor_tensor(found[:, :], rest, float(P), spare[:, :], ALU.mult, ALU.add))
                    route.then(dve.scalar_tensor_tensor(spare[:, :], found[:, :], 0.5, own_row[:, :],
                                                        ALU.is_lt, ALU.mult))
                    dve.scalar_tensor_tensor(target[:, :], found[:, :], float(-P), spare[:, :], ALU.add, ALU.add)\
                       .then_inc(table_link, 1)
                    dve.wait_ge(table_link, l + 1)
                    route.then(dve.tensor_scalar(spare[:, :], found[:, :], float(NT + P) - 0.5, float(-NT),
                                                 ALU.is_ge, ALU.mult))
                    route.then(dve.tensor_scalar(found[:, :], found[:, :], float(-P), 0.0, ALU.add, ALU.max))
                    dve.tensor_tensor(source[:, :], found[:, :], spare[:, :], ALU.add).then_inc(table_done, 1)

                slots_of()
                taken = 0
                for k in range(SHARED):
                    if k == done[0]:
                        shared_steps(1)
                    for _ in range(PLAN[l].get(k, 0)):
                        batch(taken)
                        taken += 1
                    if k == TABLE_STEP[l]:
                        table()
                    if k == EXPERTS_STEP[l]:
                        experts()

                def gated_routed(s):
                    if s.past(2):
                        dve.wait_ge(hT_psum, s.i + (TILES_R * l - 1))
                    gated(hr[:, s.u % 2, :], s, first_routed[l])

                def copy_xT(s):
                    if s.u % GT:
                        return
                    g, par = s.over(GT), s.u // GT
                    dve.wait_ge(xT_psum, g + (GROUPS * l + 1))
                    if s.past(2 * GT):
                        dve.wait_ge(u_full, s.i + (first_routed[l] - GT))
                    flat = "p t c -> p (t c)"
                    dve.tensor_copy(xTH[:, par, :, :].rearrange(flat), psT[:, :]).then_inc(xT_link, 1)
                    dve.wait_ge(xT_link, g + (GROUPS * l + 1))
                    dve.tensor_tensor(xTL[:, par, :, :].rearrange(flat), psT[:, :],
                                      xTH[:, par, :, :].rearrange(flat).bitcast(fp32), ALU.subtract)\
                       .then_inc(xT_done, 1)

                def copy_y_last(par, t):
                    dve.wait_ge(y_psum, TILES_R * (l + 1) - GT + t + 1)
                    if t == 0:
                        dve.wait_ge(y_sent[par], 16 * GT * (GROUPS // 2 * (l + 1) - 1))
                    return dve.tensor_copy(yout[:, par, t, :], last_y[t % 2][:, t * D:(t + 1) * D])

                def copy_y(s):
                    if isinstance(s.i, int) and TILES_R - GT <= s.i < TILES_R - 1:
                        copy_y_last(s.u // GT, s.u % GT).then_inc(y_part, 1)
                    if s.u % GT != GT - 1:
                        return
                    g, par = s.over(GT), s.u // GT
                    if isinstance(s.i, int) and s.i == TILES_R - 1:
                        copy_y_last(par, GT - 1).then_inc(y_done, 1)
                        return
                    dve.wait_ge(y_psum, s.i + (TILES_R * l + 1))
                    if s.past(2 * GT):
                        dve.wait_ge(y_sent[par], 16 * GT * (s.over(2 * GT) + l * GROUPS // 2))
                    dve.tensor_copy(yout[:, par, :, :].rearrange("p t d -> p (t d)"), psY[:, :]).then_inc(y_done, 1)

                def add_shared_last():
                    add_shared(CHUNKS - 1)

                pipelined(dve, [(gated_routed, 2), (copy_y, 4), (copy_xT, 0)], TILES_R, 2 * GT,
                          at={1: add_shared_last})

                if l == 1:
                    continue

                def at_statistics(s):
                    dve.wait_ge(routed_added, s.i + 1)
                    for t in range(TB):
                        i = dve.bn_stats(at_stats[:, s.u, t, :],
                                         X[:, bass.ds(s.i * TB + t, 1), :].rearrange("p a d -> p (a d)"))
                    i.then_inc(at_link, 1)

                def at_aggregate(s):
                    wait_apart(dve, at_link, s.i * 2 + 1)
                    if s.past(2):
                        wait_apart(dve, rms_terms, s.i - 1)
                    for t in range(TB):
                        i = dve.bn_aggr(at_mv[:, s.u, t, :], at_stats[:, s.u, t, :])
                    i.then_inc(at_link, 1)
                    dve.wait_ge(at_link, s.i * 2 + 2)
                    dve.tensor_scalar(at_var[:, s.u, 1, :], at_mv[:, s.u, :, 1], 1.0 + RMS_EPS, RMS_EPS * LN_EPS,
                                      ALU.mult, ALU.add)
                    dve.tensor_scalar(at_var[:, s.u, 0, :], at_mv[:, s.u, :, 1], LN_EPS, None, ALU.add)\
                       .then_inc(at_stat, 1)

                def at_normalise(s):
                    dve.wait_ge(at_scaled, s.i + 1)
                    if s.past(2):
                        dve.wait_ge(anT_psum, s.i - 1)
                        dve.wait_ge(xres_done, s.i - 1)
                    for t in range(TB):
                        xt = X[:, bass.ds(s.i * TB + t, 1), :].rearrange("p a d -> p (a d)")
                        i = dve.tensor_scalar(xn[:, s.u, t, :], xt, at_mv[:, s.u, t, 0:1],
                                              at_rstd[:, s.u, t:t + 1], ALU.subtract, ALU.mult)
                    i.then_inc(xn_ready, 1)

                def weigh_v(s):
                    dve.wait_ge(w_done, s.i + 1)
                    for t in range(TB):
                        i = dve.scalar_tensor_tensor(wkv[:, s.u, t, 1, :], psQKV[s.u][:, t, 2 * D:3 * D],
                                                     at_fac[:, s.u, 2, t:t + 1], wkv[:, s.u, t, 0, :],
                                                     ALU.mult, ALU.mult)
                    i.then_inc(kv_done, 1)

                def invert(s):
                    dve.wait_ge(den_done, s.i + 1)
                    dve.reciprocal(rec[:, s.u, :, :], den[:, s.u, :, :]).then_inc(y_link, 1)

                def scale_q(s):
                    dve.wait_ge(y_link, s.i * 2 + 1)
                    dve.scalar_tensor_tensor(ysc[:, s.u, :, :], tq[:, s.u, :, :], 1.0, rec[:, s.u, :, :],
                                             ALU.add, ALU.mult).then_inc(y_link, 1)

                def attend(s):
                    sums = psU[:, 0, :].rearrange("p (t a d) -> p t a d", t=TB, a=2)
                    dve.wait_ge(y_link, s.i * 2 + 2)
                    if s.past(2):
                        dve.wait_ge(yT_psum, s.i - 1)
                    dve.tensor_tensor(ya[:, s.u, :, :], ysc[:, s.u, :, :], sums[:, :, 1, :], ALU.mult)\
                       .then_inc(ya_done, 1)

                def gate_g(s):
                    dve.wait_ge(tg_done, s.i + 1)
                    dve.scalar_tensor_tensor(ag[:, s.u, :], tg[:, s.u, :], 1.0, psU[:, 1, 256:512],
                                             ALU.add, ALU.mult).then_inc(h_link, 1)

                def gate_u(s):
                    dve.wait_ge(h_link, s.i + 1)
                    if s.past(2):
                        dve.wait_ge(at_psum, s.i - 1)
                    dve.tensor_tensor(ha[:, s.u, :], ag[:, s.u, :], psU[:, 1, 0:256], ALU.mult)\
                       .then_inc(ha_done, 1)

                def add_attention(s):
                    dve.wait_ge(at_psum, s.i + 1)
                    dve.wait_ge(xres_done, s.i + 1)
                    xs = X[:, bass.ds(s.i * TB, TB), :].rearrange("p t d -> p (t d)")
                    dve.scalar_tensor_tensor(xs, psY[:, 0:TB * D], 0.5, xs, ALU.mult, ALU.add)\
                       .then_inc(at_added, 1)

                stages = {"weigh_v": weigh_v, "gate_u": gate_u, "add_attention": add_attention,
                          "at_normalise": at_normalise, "at_statistics": at_statistics, "attend": attend,
                          "at_aggregate": at_aggregate, "invert": invert, "scale_q": scale_q, "gate_g": gate_g}

                def ln_ahead(chunks):
                    def run():
                        for c in chunks:
                            stats(1, Step.of(c, 2))
                            if c > 0:
                                normalise(1, Step.of(c - 1, 2))
                    return run

                pipelined(dve, [(stages[n], d) for n, d in DVE_STAGES], BATCHES, 2,
                          at={k: ln_ahead(chunks) for k, chunks in LN_STEPS.items()})

            dve.wait_ge(sh_added, 2 * CHUNKS)
            n = 0
            for c in range(CHUNKS):
                if c in POOL_CHUNKS:
                    continue
                dve.wait_ge(yf_in[c], 16 * TOPK)
                n += 1
                for k in range(TOPK):
                    for t in range(c * CH, (c + 1) * CH):
                        i = dve.scalar_tensor_tensor(X[:, t, :], YF[:, k, t, :], gates[:, k, t:t + 1], X[:, t, :],
                                                     ALU.mult, ALU.add)
                    if k == 0:
                        i.then_inc(last_link, 1)
                        dve.wait_ge(last_link, n)
                i.then_inc(last_added, 1)

        @block.scalar
        def _(act):
            act.wait_ge(consts, CONSTS)
            for l in range(2):
                def copy_xnT(s):
                    act.wait_ge(xnT_psum, s.i + (CHUNKS * l + 1))
                    act.activation(XNT[:, bass.ds(s.i * CH * P, CH * P)], psH[:, s.u, :], ACT.Copy)\
                       .then_inc(xnT_done, 1)

                def copy_logits(s):
                    act.wait_ge(logits_done, s.i + (CHUNKS * l + 1))
                    act.activation(logit[:, bass.ds(s.i * CH, CH), :],
                                   psY[:, :].rearrange("p (t e) -> p t e", t=CH)[:, :, 0:E], ACT.Copy)\
                       .then_inc(logits_out, 1)

                def high_xnT(s):
                    act.wait_ge(logits_done, s.i + (CHUNKS * l + 1))
                    chunk = bass.ds(s.i * CH * P, CH * P)
                    act.activation(XNTH[:, chunk], XNT[:, chunk], ACT.Copy).then_inc(xnT_high, 1)

                if l == 0:
                    act.wait_ge(small_in, 64)
                    act.activation(W13SH[:, :, :], W13S[:, :, :], ACT.Copy).then_inc(ws_high, 1)
                def silu_of(s, base):
                    act.wait_ge(g_full, s.i + (base + 1))
                    if s.first + base >= 2:
                        act.wait_ge(h_done, s.i + (base - 1))
                    act.activation(silu[:, s.u % 2, :], psG[:, s.u % 2, :], ACT.Silu).then_inc(silu_done, 1)

                def silu_shared(k):
                    silu_of(Step.of(k, 2), first_shared[l])

                def pairs(b):
                    act.wait_ge(tile_made, BATCHES_P * l + b + 1)
                    if b >= DEEP:
                        act.wait_ge(batch_used, BATCHES_P * l + b - DEEP + 1)
                    act.activation(pair[:, b % DEEP, :, 0, :], in_tile[:, b % 2, :, :], ACT.Copy,
                                   scale=partition[:, 0:1])
                    for m in range(BATCH):
                        i = act.activation(pair[:, b % DEEP, m, 1, :], in_tile[:, b % 2, m, :], ACT.Copy,
                                           scale=float(b * BATCH + m + 1))
                    i.then_inc(pair_made, 1)

                taken = 0
                for c in range(CHUNKS + 2):
                    if c < CHUNKS:
                        copy_xnT(Step.of(c, 2))
                    if 1 <= c <= CHUNKS:
                        copy_logits(Step.of(c - 1, 2))
                    if c >= 2:
                        high_xnT(Step.of(c - 2, 2))
                    for _ in range(EARLY[l].get(c, 0)):
                        silu_shared(taken)
                        taken += 1
                act.wait_ge(shifted, l + 1)
                act.activation(prob[:, :, :], cand[:, :, :], ACT.Exp).then_inc(expd, 1)
                batches = 0
                for k in range(taken, SHARED):
                    silu_shared(k)
                    for _ in range(PLAN[l].get(k, 0)):
                        pairs(batches)
                        batches += 1

                def copy_hT(s):
                    act.wait_ge(hT_psum, s.i + (TILES_R * l + 1))
                    if s.past(2):
                        act.wait_ge(y_psum, s.i + (TILES_R * l - 1))
                    act.activation(hT[:, s.u % 2, :, :].rearrange("p j c -> p (j c)"), psH[:, s.u % 2, :],
                                   ACT.Copy).then_inc(hT_done, 1)

                pipelined(act, [(lambda s: silu_of(s, first_routed[l]), 0), (copy_hT, 1)], TILES_R, 2)

                if l == 1:
                    by_pool = 0
                    for c in range(CHUNKS):
                        if c in POOL_CHUNKS:
                            by_pool += 1
                            act.wait_ge(last_added_pool, by_pool)
                        else:
                            act.wait_ge(last_added, c + 1 - by_pool)
                        chunk = slice(c * CH, (c + 1) * CH)
                        act.dma_start(out_v[:, chunk, :], X[:, chunk, :]).then_inc(out_sent, 16)
                    act.wait_ge(out_sent, 16 * CHUNKS)
                    continue

                def gate_results(s):
                    act.wait_ge(y_in[s.u % 4], 16 * TOPK * (s.over(4) + 1))
                    for k in range(TOPK):
                        for t in range(TB):
                            ys = Y[:, s.u % 4, k, t, :]
                            i = act.activation(ys, ys, ACT.Copy, scale=gates[:, k, bass.ds(s.i * TB + t, 1)])
                    i.then_inc(y_scaled, 1)

                def copy_anT(s):
                    act.wait_ge(anT_psum, s.i + 1)
                    if s.past(2):
                        act.wait_ge(qkv_psum, s.i - 1)
                    act.activation(anT[:, s.u % 2, :], psT[:, 0:TB * P], ACT.Copy).then_inc(anT_done, 1)

                def squares(s):
                    act.wait_ge(qkv_psum, s.i + 1)
                    if s.past(2):
                        act.wait_ge(qk_scaled, s.i - 1)
                    for a in range(2):
                        for t in range(TB):
                            i = act.activation(sq[:, a, t, :], psQKV[s.u % 2][:, t, a * D:(a + 1) * D], ACT.Square,
                                               scale=(2 - a) / D ** 0.5, accum_out=qk_ss[:, s.u % 2, a, t:t + 1])
                    i.then_inc(ss_done, 1)

                def weights(s):
                    act.wait_ge(qk_scaled, s.i + 1)
                    if s.past(2):
                        act.wait_ge(ya_done, s.i - 1)
                    for t in range(TB):
                        act.activation(wkv[:, s.u % 2, t, 0, :], psQKV[s.u % 2][:, t, D:2 * D], ACT.Exp,
                                       scale=at_fac[:, s.u % 2, 1, t:t + 1])
                    for t in range(TB):
                        i = act.activation(tq[:, s.u % 2, t, :], psQKV[s.u % 2][:, t, 0:D], ACT.Tanh,
                                           scale=at_fac[:, s.u % 2, 0, t:t + 1])
                    i.then_inc(w_done, 1)

                def denominator(s):
                    act.wait_ge(cum_psum, s.i + 1)
                    if s.past(2):
                        act.wait_ge(ya_done, s.i - 1)
                    sums = psU[:, 0, :].rearrange("p (t a d) -> p t a d", t=TB, a=2)
                    act.activation(den[:, s.u % 2, :, :], sums[:, :, 0, :], ACT.Copy, scale=2.0, bias=2e-6)\
                       .then_inc(den_done, 1)

                def copy_yT(s):
                    act.wait_ge(yT_psum, s.i + 1)
                    if s.past(2):
                        act.wait_ge(uv_psum, s.i - 1)
                    act.activation(yT[:, s.u % 2, :], psT[:, TB * P:2 * TB * P], ACT.Copy).then_inc(yT_done, 1)

                def tanh_g(s):
                    act.wait_ge(uv_psum, s.i + 1)
                    act.activation(tg[:, s.u % 2, :], psU[:, 1, 256:512], ACT.Tanh, scale=0.5).then_inc(tg_done, 1)

                stages = {"copy_yT": copy_yT, "tanh_g": tanh_g, "weights": weights, "copy_anT": copy_anT,
                          "squares": squares, "denominator": denominator, "gate_results": gate_results}
                pipelined(act, [(stages[n], d) for n, d in ACT_STAGES], BATCHES, 4)

        @block.tensor
        def _(pe):
            pe.wait_ge(consts, CONSTS)
            pe.wait_ge(small_in, 64)

            def product(out, a_high, a_low, b_high, b_low):
                pe.matmul(out, a_high, b_high, start=True, stop=False)
                pe.matmul(out, a_high, b_low, start=False, stop=False)
                return pe.matmul(out, a_low, b_high, start=False, stop=True)

            entries = {}

            def table_entry(l, s):
                key = (l, s.first, isinstance(s.r, int))
                if key not in entries:
                    entries[key] = pe.value_load(w_off[0:1, bass.ds(s.i, 1)], min_val=0, max_val=(E - 1) * F)
                return entries[key]

            for l in range(2):
                def in_shared(s):
                    f = s.u % FT
                    if l == 0 and s.i == 0:
                        pe.wait_ge(ws_split, 1)
                    if f == 0:
                        pe.wait_ge(xnT_split, s.over(FT) + (CHUNKS * l + 1))
                    chunk = bass.ds(s.over(FT) * CH * P, CH * P)
                    tile = slice(f * P, (f + 1) * P)
                    if s.past(2):
                        pe.wait_ge(silu_done, s.i + (first_shared[l] - 1))
                    product(psG[:, s.u % 2, :], W13SH[:, 0, tile], W13SL[:, 0, tile], XNTH[:, chunk], XNTL[:, chunk])\
                        .then_inc(g_full, 1)
                    if s.past(2):
                        pe.wait_ge(h_done, s.i + (first_shared[l] - 1))
                    product(psU[:, s.u % 2, :], W13SH[:, 1, tile], W13SL[:, 1, tile], XNTH[:, chunk], XNTL[:, chunk])\
                        .then_inc(u_full, 1)

                taken = 0
                if l == 1:
                    pe.wait_ge(at_added, BATCHES)
                for c in range(CHUNKS + 1):
                    if c < CHUNKS:
                        pe.wait_ge(xn_done, CHUNKS * l + c + 1)
                        if c >= 2:
                            pe.wait_ge(xnT_done, CHUNKS * l + c - 1)
                        for t in range(CH):
                            i = pe.transpose(psH[:, c % 2, t * P:(t + 1) * P], XN[:, c * CH + t, :], ident[:, :])
                        i.then_inc(xnT_psum, 1)
                    if c > 0:
                        pe.wait_ge(xnT_done, CHUNKS * l + c)
                        if c > 1:
                            pe.wait_ge(logits_out, CHUNKS * l + c - 1)
                        for t in range(CH):
                            tok = ((c - 1) * CH + t) * P
                            i = pe.matmul(psY[:, t * P:(t + 1) * P], XNT[:, tok:tok + P], GATE[:, :],
                                          start=True, stop=True)
                        i.then_inc(logits_done, 1)
                    for _ in range(EARLY[l].get(c, 0)):
                        in_shared(Step.of(taken, 2 * FT))
                        taken += 1

                def out_shared(s):
                    if s.u % FT:
                        return
                    c, par = s.over(FT), s.u // FT
                    pe.wait_ge(h_done, s.i + (first_shared[l] + FT))
                    if s.past(2 * FT):
                        pe.wait_ge(sh_added, c + (CHUNKS * l - 1))
                    for t in range(CH):
                        for f in range(FT):
                            i = pe.matmul(psH[:, par, t * D:(t + 1) * D], hs[:, par, f, t * P:(t + 1) * P],
                                          W2S[:, f, :], start=(f == 0), stop=(f == FT - 1))
                    i.then_inc(sh_full, 1)

                def rank():
                    pe.wait_ge(picked, l + 1)
                    flat = chosen16[:, :, :].rearrange("p i e -> p (i e)")
                    pe.matmul(psY[:, 0:TILES * E], before[:, :], flat, start=True, stop=True)
                    pe.matmul(psY[:, TILES * E:2 * TILES * E], ones16[:, :], flat, start=True, stop=True)\
                      .then_inc(ranked, 1)

                def batch(b):
                    pe.wait_ge(place_made, BATCHES_P * l + b + 1)
                    pe.wait_ge(pair_made, BATCHES_P * l + b + 1)
                    for m in range(BATCH):
                        i = pe.matmul(psT[:, 0:2 * TILES_R], at_place[:, b % DEEP, m, :],
                                      pair[:, b % DEEP, m, :, :].rearrange("p a j -> p (a j)"),
                                      start=(b + m == 0), stop=(b == BATCHES_P - 1 and m == BATCH - 1))
                    i.then_inc(batch_used, 1)

                batches = 0
                for k in range(taken, SHARED + 1):
                    for _ in range(PLAN[l].get(k - PLAN_LAG, 0)):
                        batch(batches)
                        batches += 1
                    if k < SHARED:
                        in_shared(Step.of(k, 2 * FT))
                    if k == RANK_STEP[l]:
                        rank()
                    if 5 <= k < SHARED + 1:
                        out_shared(Step.of(k - 5, 2 * FT))
                pe.wait_ge(w_off_done, l + 1)
                pe.wait_ge(experts_in, 48)
                pe.wait_ge(w_split, 2 * WPARTS)
                pe.wait_ge(ranks_read, l + 1)

                def transpose_rows(s):
                    if s.u % GT:
                        return
                    g, par = s.over(GT), s.u // GT
                    pe.wait_ge(rows_in[par], 16 * GT * (s.over(2 * GT) + (l * GROUPS // 2 + 1)))
                    if s.past(2):
                        pe.wait_ge(xT_done, g + GROUPS * l)
                    for t in range(GT):
                        i = pe.transpose(psT[:, t * P:(t + 1) * P], rows[:, par, t, :], ident[:, :])
                    i.then_inc(xT_psum, 1)

                def in_routed(s):
                    par = s.u // GT
                    high, low = xTH[:, par, s.u % GT, :], xTL[:, par, s.u % GT, :]
                    cols = bass.ds(table_entry(l, s), F)
                    if s.u % GT == 0:
                        pe.wait_ge(xT_done, s.over(GT) + (GROUPS * l + 1))
                    pe.wait_ge(silu_done, s.i + (first_routed[l] - 1))
                    product(psG[:, s.u % 2, :], high, low, W13H[:, 0, cols], W13L[:, 0, cols]).then_inc(g_full, 1)
                    pe.wait_ge(h_done, s.i + (first_routed[l] - 1))
                    product(psU[:, s.u % 2, :], high, low, W13H[:, 1, cols], W13L[:, 1, cols]).then_inc(u_full, 1)

                def transpose_h(s):
                    pe.wait_ge(h_done, s.i + (first_routed[l] + 1))
                    if s.past(2):
                        pe.wait_ge(hT_done, s.i + (TILES_R * l - 1))
                    for f in range(FT):
                        i = pe.transpose(psH[:, s.u % 2, f * P:(f + 1) * P], hr[:, s.u % 2, f * P:(f + 1) * P],
                                         ident[:, :])
                    i.then_inc(hT_psum, 1)

                def out_routed(s):
                    at = table_entry(l, s)
                    pe.wait_ge(hT_done, s.i + (TILES_R * l + 1))
                    if s.u % GT == 0 and s.past(GT):
                        pe.wait_ge(y_done, s.over(GT) + GROUPS * l)
                    t = s.u % GT
                    into = psY
                    if isinstance(s.i, int) and s.i >= TILES_R - GT:
                        into = last_y[t % 2]
                        if t >= 2:
                            pe.wait_ge(y_part, (GT - 1) * l + t - 1)
                    for f in range(FT):
                        i = pe.matmul(into[:, t * D:(t + 1) * D], hT[:, s.u % 2, f, :],
                                      W2[:, bass.ds(at + f * D, D)], start=(f == 0), stop=(f == FT - 1))
                    i.then_inc(y_psum, 1)

                def out_last():
                    out_shared(Step.of(SHARED - FT, 2 * FT))

                def last_read():
                    pe.wait_ge(sh_added, CHUNKS * (l + 1))

                def look_up(s):
                    table_entry(l, s)

                pipelined(pe, [(in_routed, 2), (look_up, 1), (transpose_h, 3), (out_routed, 4), (transpose_rows, 0)],
                          TILES_R, 2 * GT, at={1: out_last, 3: last_read})
                if l == 1:
                    continue
                pe.wait_ge(attn_in, 48)

                order = [n for n, _ in PE_STAGES]
                lag = dict(PE_STAGES)
                apart = lag["transpose_y"] - lag["transpose_xn"]
                y_first = order.index("transpose_y") < order.index("transpose_xn")

                def transpose_xn(s):
                    pe.wait_ge(xn_ready, s.i + 1)
                    issued = s.i + ((1 if y_first else 0) - apart)
                    if not isinstance(issued, int) or issued > 0:
                        pe.wait_ge(yT_done, issued)
                    if s.past(1):
                        pe.wait_ge(anT_done, s.i)
                    for t in range(TB):
                        i = pe.transpose(psT[:, t * P:(t + 1) * P], xn[:, s.u, t, :], ident[:, :])
                    i.then_inc(anT_psum, 1)

                def qkv(s):
                    pe.wait_ge(anT_done, s.i + 1)
                    if s.past(2):
                        pe.wait_ge(kv_done, s.i - 1)
                    for t in range(TB):
                        i = pe.matmul(psQKV[s.u][:, t, 0:3 * D], anT[:, s.u, t * P:(t + 1) * P], WQKV[:, :],
                                      start=True, stop=True)
                    i.then_inc(qkv_psum, 1)

                def cumulate(s):
                    pe.wait_ge(kv_done, s.i + 1)
                    if s.past(1):
                        pe.wait_ge(ya_done, s.i)
                    part = [wkv[:, s.u, t, :, :].rearrange("p a d -> p (a d)") for t in range(TB)]
                    pe.matmul(psU[:, 0, 0:256], upto[:, :], part[0], start=True, stop=True)
                    pe.matmul(psU[:, 0, 256:512], ones[:, :], part[0], start=True, stop=False)
                    pe.matmul(psU[:, 0, 256:512], upto[:, :], part[1], start=False, stop=True)\
                      .then_inc(cum_psum, 1)

                def transpose_y(s):
                    pe.wait_ge(ya_done, s.i + 1)
                    issued = s.i + ((0 if y_first else 1) + apart)
                    if isinstance(issued, int):
                        issued = min(issued, BATCHES)
                    pe.wait_ge(anT_done, issued)
                    if s.past(1):
                        pe.wait_ge(yT_done, s.i)
                    for t in range(TB):
                        i = pe.transpose(psT[:, (TB + t) * P:(TB + t + 1) * P], ya[:, s.u, t, :], ident[:, :])
                    i.then_inc(yT_psum, 1)

                def swiglu(s):
                    pe.wait_ge(yT_done, s.i + 1)
                    if s.past(1):
                        pe.wait_ge(ha_done, s.i)
                    for a in range(2):
                        i = pe.matmul(psU[:, 1, a * 256:(a + 1) * 256], WSW[:, a * D:(a + 1) * D], yT[:, s.u, :],
                                      start=True, stop=True)
                    i.then_inc(uv_psum, 1)

                def project(s):
                    pe.wait_ge(ha_done, s.i + 1)
                    if s.past(1):
                        pe.wait_ge(at_added, s.i)
                    for t in range(TB):
                        i = pe.matmul(psY[:, t * D:(t + 1) * D], ha[:, s.u, t * P:(t + 1) * P], WOUT[:, :],
                                      start=True, stop=True)
                    i.then_inc(at_psum, 1)

                stages = {"project": project, "transpose_y": transpose_y, "swiglu": swiglu, "cumulate": cumulate,
                          "transpose_xn": transpose_xn, "qkv": qkv}
                pipelined(pe, [(stages[n], d) for n, d in PE_STAGES], BATCHES, 2)


_INS = ["x", "w_qkvT", "w_swigluT", "w_outT", "gateT", "w1_e", "w3_e", "w2_e", "w1_s", "w3_s", "w2_s"]


def kernel(L0_attn_x, L0_attn_w_qkv, L0_attn_w_swiglu, L0_attn_w_out, L0_ffn_gate_W, L0_ffn_w1_e,
           L0_ffn_w3_e, L0_ffn_w2_e, L0_ffn_w1_s, L0_ffn_w3_s, L0_ffn_w2_s):
    import numpy as np
    import concourse.bacc as bacc
    from concourse.bass_utils import run_bass_kernel_spmd

    def lay(a):
        return np.ascontiguousarray(a)

    x = np.asarray(L0_attn_x)
    gateT = np.zeros((D, P), np.float32)
    gateT[:, :E] = np.asarray(L0_ffn_gate_W).T
    w1, w3, w2 = (np.asarray(a) for a in (L0_ffn_w1_e, L0_ffn_w3_e, L0_ffn_w2_e))
    arrays = {
        "x": lay(x.reshape(NT, D)),
        "w_qkvT": lay(np.asarray(L0_attn_w_qkv).T),
        "w_swigluT": lay(np.asarray(L0_attn_w_swiglu).T),
        "w_outT": lay(np.asarray(L0_attn_w_out).T),
        "gateT": gateT,
        "w1_e": lay(w1.transpose(1, 0, 2).reshape(D, E * F)),
        "w3_e": lay(w3.transpose(1, 0, 2).reshape(D, E * F)),
        "w2_e": lay(w2.reshape(E, FT, P, D).transpose(2, 0, 1, 3).reshape(P, E * FT * D)),
        "w1_s": lay(np.asarray(L0_ffn_w1_s).transpose(1, 0, 2).reshape(D, F)),
        "w3_s": lay(np.asarray(L0_ffn_w3_s).transpose(1, 0, 2).reshape(D, F)),
        "w2_s": lay(np.asarray(L0_ffn_w2_s).reshape(F, D)),
    }
    nc = bacc.Bacc("TRN2", target_bir_lowering=False, num_devices=1)
    args = [nc.dram_tensor(n, list(arrays[n].shape), fp32, kind="ExternalInput").ap() for n in _INS]
    out = nc.dram_tensor("out", [NT, D], fp32, kind="ExternalOutput").ap()
    macaron(nc, *args, out)
    result = run_bass_kernel_spmd(nc, [arrays], core_ids=[0]).results[0]
    return result["out"].reshape(x.shape)
```
